# Optimizing a Trainium2 kernel written in Bass

```python
import numpy as np
import jax
import jax.numpy as jnp

def _softmax(x, axis=-1):
    return jax.nn.softmax(x, axis=axis)

def _gelu(x):
    return jax.nn.gelu(x, approximate=True)

def _silu(x):
    return jax.nn.silu(x)

def _sigmoid(x):
    return jax.nn.sigmoid(x)

def _layernorm(x, axis=-1, eps=1e-05):
    m = jnp.mean(x, axis=axis, keepdims=True)
    v = jnp.var(x, axis=axis, keepdims=True)
    return (x - m) / jnp.sqrt(v + eps)

def _scatter_add(tgt, idx, src, axis=0):
    return tgt.at[idx].add(src)

def _segment_sum(src, seg, n):
    return jax.ops.segment_sum(src, seg, n)
kernel_name = 'mk_xattn_seq_d4_seqx_r8_b24215'

def setup_inputs(seed: int=0):
    np.random.seed(seed)
    _w = jnp.asarray

    def _rec_inputs():
        import jax
        import jax.numpy as jnp
        _rk = jax.random.key(seed)
        x = -0.0002928 + 1 * jax.random.normal(jax.random.fold_in(_rk, 1), (128, 64, 128), jnp.float32)
        _lenS = 64 - jax.random.randint(jax.random.fold_in(_rk, 7), (128,), 0, max(1, 64 // 4) + 1, jnp.int32)
        _lenS2 = 64 - jax.random.randint(jax.random.fold_in(_rk, 8), (128,), 0, max(1, 64 // 4) + 1, jnp.int32)
        _ctx_1024P = jax.random.normal(jax.random.fold_in(_rk, 11), (128, 16, 128), jnp.float32)
        _ctx_1024c = jax.random.dirichlet(jax.random.fold_in(_rk, 511), 0.3 * jnp.ones((16,), jnp.float32), (128, 64))
        _ctx_1024t = jnp.einsum('bsk,bkd->bsd', _ctx_1024c, _ctx_1024P)
        _ctx_1024t = _ctx_1024t * jax.lax.rsqrt(jnp.mean(jnp.square(_ctx_1024t)) + 1e-12) * 0.953939
        ctx_1024 = -0.000494167 + 1.00018 * (_ctx_1024t + 0.3 * jax.random.normal(jax.random.fold_in(_rk, 611), (128, 64, 128), jnp.float32))
        _validS = jnp.arange(64)[None, :] < _lenS[:, None]
        _validS2 = jnp.arange(64)[None, :] < _lenS2[:, None]
        _causal = jnp.tril(jnp.ones((64, 64), dtype=bool))
        mask_1xS2_if1 = jnp.where(jnp.ones((1, 64), dtype=bool), 1, 0).astype(jnp.int32)
        return (x, ctx_1024, mask_1xS2_if1)
    x, ctx_1024, mask_1xS2_if1 = _rec_inputs()

    def _L0_xattn_setup():
        import jax, jax.numpy as jnp
        import numpy as np
        DIM = 128
        HEADS = 16
        HEAD_DIM = DIM // HEADS
        HIDDEN = int(DIM * 4.0)
        SCALE = HEAD_DIM ** (-0.5)
        EPS = 1e-05

        def _ln(x, g, b):
            m = jnp.mean(x, axis=-1, keepdims=True)
            v = jnp.mean((x - m) ** 2, axis=-1, keepdims=True)
            return (x - m) * jax.lax.rsqrt(v + EPS) * g + b

        def _split_heads(t, B, N):
            return t.reshape(B, N, HEADS, HEAD_DIM).transpose(0, 2, 1, 3)
        key = jax.random.key(seed)
        ks = jax.random.split(key, 16)
        B, Nt, Ni = (4, 128, 72)
        s = lambda fan_in: 1.0 / np.sqrt(fan_in)
        return {'x': jax.random.normal(ks[0], (B, Nt, DIM), jnp.float32), 'encoder_hidden_state': jax.random.normal(ks[1], (B, Ni, DIM), jnp.float32), 'ln1_g': jnp.ones((DIM,), jnp.float32), 'ln1_b': jnp.zeros((DIM,), jnp.float32), 'w_qkv': jax.random.uniform(ks[2], (3 * DIM, DIM), jnp.float32, -s(DIM), s(DIM)), 'w_prj1': jax.random.uniform(ks[3], (DIM, DIM), jnp.float32, -s(DIM), s(DIM)), 'b_prj1': jnp.zeros((DIM,), jnp.float32), 'ln2_g': jnp.ones((DIM,), jnp.float32), 'ln2_b': jnp.zeros((DIM,), jnp.float32), 'w_q': jax.random.uniform(ks[4], (DIM, DIM), jnp.float32, -s(DIM), s(DIM)), 'w_kv': jax.random.uniform(ks[5], (2 * DIM, DIM), jnp.float32, -s(DIM), s(DIM)), 'w_prj2': jax.random.uniform(ks[6], (DIM, DIM), jnp.float32, -s(DIM), s(DIM)), 'b_prj2': jnp.zeros((DIM,), jnp.float32), 'ln3_g': jnp.ones((DIM,), jnp.float32), 'ln3_b': jnp.zeros((DIM,), jnp.float32), 'w_fc1': jax.random.uniform(ks[7], (HIDDEN, DIM), jnp.float32, -s(DIM), s(DIM)), 'b_fc1': jnp.zeros((HIDDEN,), jnp.float32), 'w_fc2': jax.random.uniform(ks[8], (DIM, HIDDEN), jnp.float32, -s(HIDDEN), s(HIDDEN)), 'b_fc2': jnp.zeros((DIM,), jnp.float32)}
    _L0_xattn_all = _L0_xattn_setup()
    _L0_xattn_in = {k: v for k, v in _L0_xattn_all.items() if k in ('ln1_g', 'ln1_b', 'w_qkv', 'w_prj1', 'b_prj1', 'ln2_g', 'ln2_b', 'w_q', 'w_kv', 'w_prj2', 'b_prj2', 'ln3_g', 'ln3_b', 'w_fc1', 'b_fc1', 'w_fc2', 'b_fc2')}
    del _L0_xattn_all

    def _L1_xattn_setup():
        import jax, jax.numpy as jnp
        import numpy as np
        EPS = 1e-06
        ROPE_BASE = 10000.0

        def rmsnorm(x, w):
            return x * jax.lax.rsqrt(jnp.mean(x * x, axis=-1, keepdims=True) + EPS) * w

        def rope(t, offset, head_dim):
            T = t.shape[1]
            half = head_dim // 2
            inv_freq = 1.0 / ROPE_BASE ** (jnp.arange(0, half, dtype=jnp.float32) / half)
            pos = jnp.arange(T, dtype=jnp.float32) + offset
            ang = pos[:, None] * inv_freq[None, :]
            cos = jnp.concatenate([jnp.cos(ang), jnp.cos(ang)], axis=-1)[None, :, None, :]
            sin = jnp.concatenate([jnp.sin(ang), jnp.sin(ang)], axis=-1)[None, :, None, :]
            t1, t2 = (t[..., :half], t[..., half:])
            rot = jnp.concatenate([-t2, t1], axis=-1)
            return t * cos + rot * sin
        key = jax.random.key(seed)
        ks = jax.random.split(key, 6)
        B, Td, Te, d = (4, 256, 256, 128)
        s = 1.0 / np.sqrt(d)
        return {'x': jax.random.normal(ks[0], (B, Td, d), jnp.float32), 'encoder_out': jax.random.normal(ks[1], (B, Te, d), jnp.float32), 'norm_w': jnp.ones((d,), jnp.float32), 'Wq': jax.random.normal(ks[2], (d, d), jnp.float32) * s, 'Wkv': jax.random.normal(ks[3], (2 * d, d), jnp.float32) * s, 'Wo': jax.random.normal(ks[4], (d, d), jnp.float32) * s, 'decoder_offset': 0}
    _L1_xattn_all = _L1_xattn_setup()
    _L1_xattn_in = {k: v for k, v in _L1_xattn_all.items() if k in ('norm_w', 'Wq', 'Wkv', 'Wo')}
    del _L1_xattn_all

    def _L2_xattn_setup():
        import jax, jax.numpy as jnp
        import numpy as np
        NEG = 10000000000.0

        def layer_norm(x, g, b, eps):
            m = jnp.mean(x, axis=-1, keepdims=True)
            v = jnp.mean(jnp.square(x - m), axis=-1, keepdims=True)
            return (x - m) * jax.lax.rsqrt(v + eps) * g + b

        def mha(q, k, v, mask, num_heads):
            B, T, E = q.shape
            S = k.shape[1]
            D = E // num_heads
            qh = q.reshape(B, T, num_heads, D).transpose(0, 2, 1, 3)
            kh = k.reshape(B, S, num_heads, D).transpose(0, 2, 1, 3)
            vh = v.reshape(B, S, num_heads, D).transpose(0, 2, 1, 3)
            scores = jnp.einsum('bhqd,bhkd->bhqk', qh, kh) * (1.0 / np.sqrt(D))
            scores = scores * mask - (1.0 - mask) * NEG
            attn = jax.nn.softmax(scores, axis=-1)
            out = jnp.einsum('bhqk,bhkd->bhqd', attn, vh)
            return out.transpose(0, 2, 1, 3).reshape(B, T, E)
        NUM_HEADS = 16
        key = jax.random.key(seed)
        ks = jax.random.split(key, 16)
        B, T, S, E, F, H = (1, 256, 256, 128, 512, 16)
        std = 0.02
        inp = {'target': jax.random.normal(ks[0], (B, T, E), jnp.float32), 'context': jax.random.normal(ks[1], (B, S, E), jnp.float32), 'target_pad_mask': jnp.ones((B, T), jnp.int32), 'context_pad_mask': jnp.ones((B, S), jnp.int32), 'Wqkv': jax.random.normal(ks[2], (E, 3 * E), jnp.float32) * std, 'Wo1': jax.random.normal(ks[3], (E, E), jnp.float32) * (std / np.sqrt(24.0)), 'bo1': jnp.zeros((E,), jnp.float32), 'g1': jnp.ones((E,), jnp.float32), 'b1': jnp.zeros((E,), jnp.float32), 'Wq': jax.random.normal(ks[4], (E, E), jnp.float32) * std, 'Wk': jax.random.normal(ks[5], (E, E), jnp.float32) * std, 'Wv': jax.random.normal(ks[6], (E, E), jnp.float32) * std, 'Wo2': jax.random.normal(ks[7], (E, E), jnp.float32) * (std / np.sqrt(24.0)), 'bo2': jnp.zeros((E,), jnp.float32), 'g2': jnp.ones((E,), jnp.float32), 'b2': jnp.zeros((E,), jnp.float32), 'W1': jax.random.normal(ks[8], (E, F), jnp.float32) * std, 'bf1': jnp.zeros((F,), jnp.float32), 'W2': jax.random.normal(ks[9], (F, E), jnp.float32) * std, 'bf2': jnp.zeros((E,), jnp.float32), 'g3': jnp.ones((E,), jnp.float32), 'b3': jnp.zeros((E,), jnp.float32)}
        return inp
    _L2_xattn_all = _L2_xattn_setup()
    _L2_xattn_in = {k: v for k, v in _L2_xattn_all.items() if k in ('Wqkv', 'Wo1', 'bo1', 'g1', 'b1', 'Wq', 'Wk', 'Wv', 'Wo2', 'bo2', 'g2', 'b2', 'W1', 'bf1', 'W2', 'bf2', 'g3', 'b3')}
    del _L2_xattn_all

    def _L3_xattn_setup():
        import jax, jax.numpy as jnp
        import numpy as np
        B, N, M = (2, 256, 128)
        C, CTX, H = (128, 128, 16)
        D = C // H
        HID = int(C * 4.0)
        EPS = 1e-06

        def _ln(h):
            h32 = h.astype(jnp.float32)
            mu = jnp.mean(h32, axis=-1, keepdims=True)
            var = jnp.var(h32, axis=-1, keepdims=True)
            return ((h32 - mu) * jax.lax.rsqrt(var + EPS)).astype(h.dtype)

        def _sdpa(q, k, v):
            scale = 1.0 / np.sqrt(D)
            s = jnp.einsum('bqhd,bkhd->bhqk', q, k) * scale
            p = jax.nn.softmax(s, axis=-1)
            return jnp.einsum('bhqk,bkhd->bqhd', p, v)

        def _forward(x, context, Wqkv, bqkv, Wos, bos, Wq, bq, Wkv, bkv, Woc, boc, W1, b1, W2, b2):
            Bx, Nx, _ = x.shape
            Mx = context.shape[1]
            h = _ln(x)
            qkv = (h @ Wqkv + bqkv).reshape(Bx, Nx, 3, H, D)
            q, k, v = (qkv[:, :, 0], qkv[:, :, 1], qkv[:, :, 2])
            a = _sdpa(q, k, v).reshape(Bx, Nx, C)
            x = x + (a @ Wos + bos)
            h = _ln(x)
            q = (h @ Wq + bq).reshape(Bx, Nx, H, D)
            kv = (context @ Wkv + bkv).reshape(Bx, Mx, 2, H, D)
            k, v = (kv[:, :, 0], kv[:, :, 1])
            a = _sdpa(q, k, v).reshape(Bx, Nx, C)
            x = x + (a @ Woc + boc)
            h = _ln(x)
            x = x + (jax.nn.gelu(h @ W1 + b1, approximate=True) @ W2 + b2)
            return x
        key = jax.random.key(seed)
        ks = jax.random.split(key, 12)
        rn = lambda k, shape: jax.random.normal(k, shape, jnp.float32) * 0.02
        return {'x': jax.random.normal(ks[0], (B, N, C), jnp.float32), 'context': jax.random.normal(ks[1], (B, M, CTX), jnp.float32), 'Wqkv': rn(ks[2], (C, 3 * C)), 'bqkv': jnp.zeros((3 * C,), jnp.float32), 'Wos': rn(ks[3], (C, C)), 'bos': jnp.zeros((C,), jnp.float32), 'Wq': rn(ks[4], (C, C)), 'bq': jnp.zeros((C,), jnp.float32), 'Wkv': rn(ks[5], (CTX, 2 * C)), 'bkv': jnp.zeros((2 * C,), jnp.float32), 'Woc': rn(ks[6], (C, C)), 'boc': jnp.zeros((C,), jnp.float32), 'W1': rn(ks[7], (C, HID)), 'b1': jnp.zeros((HID,), jnp.float32), 'W2': rn(ks[8], (HID, C)), 'b2': jnp.zeros((C,), jnp.float32)}
    _L3_xattn_all = _L3_xattn_setup()
    _L3_xattn_in = {k: v for k, v in _L3_xattn_all.items() if k in ('Wqkv', 'bqkv', 'Wos', 'bos', 'Wq', 'bq', 'Wkv', 'bkv', 'Woc', 'boc', 'W1', 'b1', 'W2', 'b2')}
    del _L3_xattn_all
    return {'x': x, 'ctx_1024': ctx_1024, 'mask_1xS2_if1': mask_1xS2_if1, 'L0_xattn_ln1_g': _L0_xattn_in['ln1_g'], 'L0_xattn_ln1_b': _L0_xattn_in['ln1_b'], 'L0_xattn_w_qkv': _L0_xattn_in['w_qkv'], 'L0_xattn_w_prj1': _L0_xattn_in['w_prj1'], 'L0_xattn_b_prj1': _L0_xattn_in['b_prj1'], 'L0_xattn_ln2_g': _L0_xattn_in['ln2_g'], 'L0_xattn_ln2_b': _L0_xattn_in['ln2_b'], 'L0_xattn_w_q': _L0_xattn_in['w_q'], 'L0_xattn_w_kv': _L0_xattn_in['w_kv'], 'L0_xattn_w_prj2': _L0_xattn_in['w_prj2'], 'L0_xattn_b_prj2': _L0_xattn_in['b_prj2'], 'L0_xattn_ln3_g': _L0_xattn_in['ln3_g'], 'L0_xattn_ln3_b': _L0_xattn_in['ln3_b'], 'L0_xattn_w_fc1': _L0_xattn_in['w_fc1'], 'L0_xattn_b_fc1': _L0_xattn_in['b_fc1'], 'L0_xattn_w_fc2': _L0_xattn_in['w_fc2'], 'L0_xattn_b_fc2': _L0_xattn_in['b_fc2'], 'L1_xattn_norm_w': _L1_xattn_in['norm_w'], 'L1_xattn_Wq': _L1_xattn_in['Wq'], 'L1_xattn_Wkv': _L1_xattn_in['Wkv'], 'L1_xattn_Wo': _L1_xattn_in['Wo'], 'L2_xattn_Wqkv': _L2_xattn_in['Wqkv'], 'L2_xattn_Wo1': _L2_xattn_in['Wo1'], 'L2_xattn_bo1': _L2_xattn_in['bo1'], 'L2_xattn_g1': _L2_xattn_in['g1'], 'L2_xattn_b1': _L2_xattn_in['b1'], 'L2_xattn_Wq': _L2_xattn_in['Wq'], 'L2_xattn_Wk': _L2_xattn_in['Wk'], 'L2_xattn_Wv': _L2_xattn_in['Wv'], 'L2_xattn_Wo2': _L2_xattn_in['Wo2'], 'L2_xattn_bo2': _L2_xattn_in['bo2'], 'L2_xattn_g2': _L2_xattn_in['g2'], 'L2_xattn_b2': _L2_xattn_in['b2'], 'L2_xattn_W1': _L2_xattn_in['W1'], 'L2_xattn_bf1': _L2_xattn_in['bf1'], 'L2_xattn_W2': _L2_xattn_in['W2'], 'L2_xattn_bf2': _L2_xattn_in['bf2'], 'L2_xattn_g3': _L2_xattn_in['g3'], 'L2_xattn_b3': _L2_xattn_in['b3'], 'L3_xattn_Wqkv': _L3_xattn_in['Wqkv'], 'L3_xattn_bqkv': _L3_xattn_in['bqkv'], 'L3_xattn_Wos': _L3_xattn_in['Wos'], 'L3_xattn_bos': _L3_xattn_in['bos'], 'L3_xattn_Wq': _L3_xattn_in['Wq'], 'L3_xattn_bq': _L3_xattn_in['bq'], 'L3_xattn_Wkv': _L3_xattn_in['Wkv'], 'L3_xattn_bkv': _L3_xattn_in['bkv'], 'L3_xattn_Woc': _L3_xattn_in['Woc'], 'L3_xattn_boc': _L3_xattn_in['boc'], 'L3_xattn_W1': _L3_xattn_in['W1'], 'L3_xattn_b1': _L3_xattn_in['b1'], 'L3_xattn_W2': _L3_xattn_in['W2'], 'L3_xattn_b2': _L3_xattn_in['b2']}

def reference(x, ctx_1024, mask_1xS2_if1, L0_xattn_ln1_g, L0_xattn_ln1_b, L0_xattn_w_qkv, L0_xattn_w_prj1, L0_xattn_b_prj1, L0_xattn_ln2_g, L0_xattn_ln2_b, L0_xattn_w_q, L0_xattn_w_kv, L0_xattn_w_prj2, L0_xattn_b_prj2, L0_xattn_ln3_g, L0_xattn_ln3_b, L0_xattn_w_fc1, L0_xattn_b_fc1, L0_xattn_w_fc2, L0_xattn_b_fc2, L1_xattn_norm_w, L1_xattn_Wq, L1_xattn_Wkv, L1_xattn_Wo, L2_xattn_Wqkv, L2_xattn_Wo1, L2_xattn_bo1, L2_xattn_g1, L2_xattn_b1, L2_xattn_Wq, L2_xattn_Wk, L2_xattn_Wv, L2_xattn_Wo2, L2_xattn_bo2, L2_xattn_g2, L2_xattn_b2, L2_xattn_W1, L2_xattn_bf1, L2_xattn_W2, L2_xattn_bf2, L2_xattn_g3, L2_xattn_b3, L3_xattn_Wqkv, L3_xattn_bqkv, L3_xattn_Wos, L3_xattn_bos, L3_xattn_Wq, L3_xattn_bq, L3_xattn_Wkv, L3_xattn_bkv, L3_xattn_Woc, L3_xattn_boc, L3_xattn_W1, L3_xattn_b1, L3_xattn_W2, L3_xattn_b2):
    import jax
    import jax.numpy as jnp

    def _L0_xattn_ref(x, encoder_hidden_state, ln1_g, ln1_b, w_qkv, w_prj1, b_prj1, ln2_g, ln2_b, w_q, w_kv, w_prj2, b_prj2, ln3_g, ln3_b, w_fc1, b_fc1, w_fc2, b_fc2):
        import jax, jax.numpy as jnp
        import numpy as np
        DIM = 128
        HEADS = 16
        HEAD_DIM = DIM // HEADS
        HIDDEN = int(DIM * 4.0)
        SCALE = HEAD_DIM ** (-0.5)
        EPS = 1e-05

        def _ln(x, g, b):
            m = jnp.mean(x, axis=-1, keepdims=True)
            v = jnp.mean((x - m) ** 2, axis=-1, keepdims=True)
            return (x - m) * jax.lax.rsqrt(v + EPS) * g + b

        def _split_heads(t, B, N):
            return t.reshape(B, N, HEADS, HEAD_DIM).transpose(0, 2, 1, 3)
        B, Nt, C = x.shape
        Ni = encoder_hidden_state.shape[1]
        h = _ln(x, ln1_g, ln1_b)
        qkv = h @ w_qkv.T
        q, k, v = jnp.split(qkv, 3, axis=-1)
        q, k, v = (_split_heads(q, B, Nt), _split_heads(k, B, Nt), _split_heads(v, B, Nt))
        attn = jnp.einsum('bhqd,bhkd->bhqk', q, k) * SCALE
        causal = jnp.tril(jnp.ones((Nt, Nt), bool))
        attn = jnp.where(causal, attn, -jnp.inf)
        attn = jax.nn.softmax(attn, axis=-1)
        o = jnp.einsum('bhqk,bhkd->bhqd', attn, v).transpose(0, 2, 1, 3).reshape(B, Nt, C)
        x = x + o @ w_prj1.T + b_prj1
        h = _ln(x, ln2_g, ln2_b)
        q = _split_heads(h @ w_q.T, B, Nt)
        kv = encoder_hidden_state @ w_kv.T
        k, v = jnp.split(kv, 2, axis=-1)
        k, v = (_split_heads(k, B, Ni), _split_heads(v, B, Ni))
        attn = jnp.einsum('bhqd,bhkd->bhqk', q, k) * SCALE
        attn = jax.nn.softmax(attn, axis=-1)
        o = jnp.einsum('bhqk,bhkd->bhqd', attn, v).transpose(0, 2, 1, 3).reshape(B, Nt, C)
        x = x + o @ w_prj2.T + b_prj2
        h = _ln(x, ln3_g, ln3_b)
        h = jax.nn.gelu(h @ w_fc1.T + b_fc1, approximate=False)
        x = x + h @ w_fc2.T + b_fc2
        return x

    def _L1_xattn_ref(x, encoder_out, norm_w, Wq, Wkv, Wo, decoder_offset):
        import jax, jax.numpy as jnp
        import numpy as np
        EPS = 1e-06
        ROPE_BASE = 10000.0

        def rmsnorm(x, w):
            return x * jax.lax.rsqrt(jnp.mean(x * x, axis=-1, keepdims=True) + EPS) * w

        def rope(t, offset, head_dim):
            T = t.shape[1]
            half = head_dim // 2
            inv_freq = 1.0 / ROPE_BASE ** (jnp.arange(0, half, dtype=jnp.float32) / half)
            pos = jnp.arange(T, dtype=jnp.float32) + offset
            ang = pos[:, None] * inv_freq[None, :]
            cos = jnp.concatenate([jnp.cos(ang), jnp.cos(ang)], axis=-1)[None, :, None, :]
            sin = jnp.concatenate([jnp.sin(ang), jnp.sin(ang)], axis=-1)[None, :, None, :]
            t1, t2 = (t[..., :half], t[..., half:])
            rot = jnp.concatenate([-t2, t1], axis=-1)
            return t * cos + rot * sin
        B, Td, d = x.shape
        Te = encoder_out.shape[1]
        H = 16
        D = d // H
        residual = x
        h = rmsnorm(x, norm_w)
        q = (h @ Wq.T).reshape(B, Td, H, D)
        kv = (encoder_out @ Wkv.T).reshape(B, Te, 2, H, D)
        k, v = (kv[:, :, 0], kv[:, :, 1])
        q = rope(q, decoder_offset, D)
        k = rope(k, 0, D)
        scale = 1.0 / np.sqrt(D)
        scores = jnp.einsum('bqhd,bkhd->bhqk', q, k) * scale
        attn = jax.nn.softmax(scores, axis=-1)
        out = jnp.einsum('bhqk,bkhd->bqhd', attn, v).reshape(B, Td, d)
        out = out @ Wo.T
        return residual + out

    def _L2_xattn_ref(target, context, target_pad_mask, context_pad_mask, Wqkv, Wo1, bo1, g1, b1, Wq, Wk, Wv, Wo2, bo2, g2, b2, W1, bf1, W2, bf2, g3, b3):
        import jax, jax.numpy as jnp
        import numpy as np
        NEG = 10000000000.0

        def layer_norm(x, g, b, eps):
            m = jnp.mean(x, axis=-1, keepdims=True)
            v = jnp.mean(jnp.square(x - m), axis=-1, keepdims=True)
            return (x - m) * jax.lax.rsqrt(v + eps) * g + b

        def mha(q, k, v, mask, num_heads):
            B, T, E = q.shape
            S = k.shape[1]
            D = E // num_heads
            qh = q.reshape(B, T, num_heads, D).transpose(0, 2, 1, 3)
            kh = k.reshape(B, S, num_heads, D).transpose(0, 2, 1, 3)
            vh = v.reshape(B, S, num_heads, D).transpose(0, 2, 1, 3)
            scores = jnp.einsum('bhqd,bhkd->bhqk', qh, kh) * (1.0 / np.sqrt(D))
            scores = scores * mask - (1.0 - mask) * NEG
            attn = jax.nn.softmax(scores, axis=-1)
            out = jnp.einsum('bhqk,bhkd->bhqd', attn, vh)
            return out.transpose(0, 2, 1, 3).reshape(B, T, E)
        NUM_HEADS = 16
        B, T, E = target.shape
        S = context.shape[1]
        tpad = target_pad_mask.astype(target.dtype)
        cpad = context_pad_mask.astype(target.dtype)
        causal = (jnp.arange(T)[:, None] >= jnp.arange(T)[None, :]).astype(target.dtype)
        self_mask = causal[None, None, :, :] * tpad[:, None, None, :]
        q, k, v = jnp.split(target @ Wqkv, 3, axis=-1)
        x = mha(q, k, v, self_mask, NUM_HEADS) @ Wo1 + bo1
        target = layer_norm(x + target, g1, b1, 1e-05)
        cross_mask = jnp.broadcast_to(cpad[:, None, None, :], (B, 1, 1, S))
        x = mha(target @ Wq, context @ Wk, context @ Wv, cross_mask, NUM_HEADS) @ Wo2 + bo2
        target = layer_norm(x + target, g2, b2, 1e-05)
        h = jax.nn.gelu(target @ W1 + bf1, approximate=False)
        x = h @ W2 + bf2
        return layer_norm(x + target, g3, b3, 1e-06)

    def _L3_xattn_ref(x, context, Wqkv, bqkv, Wos, bos, Wq, bq, Wkv, bkv, Woc, boc, W1, b1, W2, b2):
        import jax, jax.numpy as jnp
        import numpy as np
        B, N, M = (2, 256, 128)
        C, CTX, H = (128, 128, 16)
        D = C // H
        HID = int(C * 4.0)
        EPS = 1e-06

        def _ln(h):
            h32 = h.astype(jnp.float32)
            mu = jnp.mean(h32, axis=-1, keepdims=True)
            var = jnp.var(h32, axis=-1, keepdims=True)
            return ((h32 - mu) * jax.lax.rsqrt(var + EPS)).astype(h.dtype)

        def _sdpa(q, k, v):
            scale = 1.0 / np.sqrt(D)
            s = jnp.einsum('bqhd,bkhd->bhqk', q, k) * scale
            p = jax.nn.softmax(s, axis=-1)
            return jnp.einsum('bhqk,bkhd->bqhd', p, v)

        def _forward(x, context, Wqkv, bqkv, Wos, bos, Wq, bq, Wkv, bkv, Woc, boc, W1, b1, W2, b2):
            Bx, Nx, _ = x.shape
            Mx = context.shape[1]
            h = _ln(x)
            qkv = (h @ Wqkv + bqkv).reshape(Bx, Nx, 3, H, D)
            q, k, v = (qkv[:, :, 0], qkv[:, :, 1], qkv[:, :, 2])
            a = _sdpa(q, k, v).reshape(Bx, Nx, C)
            x = x + (a @ Wos + bos)
            h = _ln(x)
            q = (h @ Wq + bq).reshape(Bx, Nx, H, D)
            kv = (context @ Wkv + bkv).reshape(Bx, Mx, 2, H, D)
            k, v = (kv[:, :, 0], kv[:, :, 1])
            a = _sdpa(q, k, v).reshape(Bx, Nx, C)
            x = x + (a @ Woc + boc)
            h = _ln(x)
            x = x + (jax.nn.gelu(h @ W1 + b1, approximate=True) @ W2 + b2)
            return x
        return _forward(x, context, Wqkv, bqkv, Wos, bos, Wq, bq, Wkv, bkv, Woc, boc, W1, b1, W2, b2)
    x = _L0_xattn_ref(x, ctx_1024, L0_xattn_ln1_g, L0_xattn_ln1_b, L0_xattn_w_qkv, L0_xattn_w_prj1, L0_xattn_b_prj1, L0_xattn_ln2_g, L0_xattn_ln2_b, L0_xattn_w_q, L0_xattn_w_kv, L0_xattn_w_prj2, L0_xattn_b_prj2, L0_xattn_ln3_g, L0_xattn_ln3_b, L0_xattn_w_fc1, L0_xattn_b_fc1, L0_xattn_w_fc2, L0_xattn_b_fc2)
    x = _L1_xattn_ref(x, ctx_1024, L1_xattn_norm_w, L1_xattn_Wq, L1_xattn_Wkv, L1_xattn_Wo, 0)
    x = _L2_xattn_ref(x, ctx_1024, mask_1xS2_if1, mask_1xS2_if1, L2_xattn_Wqkv, L2_xattn_Wo1, L2_xattn_bo1, L2_xattn_g1, L2_xattn_b1, L2_xattn_Wq, L2_xattn_Wk, L2_xattn_Wv, L2_xattn_Wo2, L2_xattn_bo2, L2_xattn_g2, L2_xattn_b2, L2_xattn_W1, L2_xattn_bf1, L2_xattn_W2, L2_xattn_bf2, L2_xattn_g3, L2_xattn_b3)
    x = _L3_xattn_ref(x, ctx_1024, L3_xattn_Wqkv, L3_xattn_bqkv, L3_xattn_Wos, L3_xattn_bos, L3_xattn_Wq, L3_xattn_bq, L3_xattn_Wkv, L3_xattn_bkv, L3_xattn_Woc, L3_xattn_boc, L3_xattn_W1, L3_xattn_b1, L3_xattn_W2, L3_xattn_b2)
    return x

_drawn_inputs = setup_inputs


def setup_inputs(seed=0):
    import zlib

    import numpy as np

    out = dict(_drawn_inputs(seed))
    spreads = {'L0_xattn_ln1_g': (1.0, 0.6),
     'L0_xattn_ln1_b': (0.0, 0.269),
     'L0_xattn_b_prj1': (0.0, 0.1),
     'L0_xattn_ln2_g': (1.0, 0.6),
     'L0_xattn_ln2_b': (0.0, 0.8),
     'L0_xattn_b_prj2': (0.0, 0.1),
     'L0_xattn_ln3_g': (1.0, 0.2),
     'L0_xattn_ln3_b': (0.0, 0.416),
     'L0_xattn_b_fc1': (0.0, 0.1),
     'L0_xattn_b_fc2': (0.0, 0.1),
     'L1_xattn_norm_w': (1.0, 0.2),
     'L2_xattn_bo1': (0.0, 0.1),
     'L2_xattn_g1': (1.0, 0.2),
     'L2_xattn_b1': (0.0, 0.1),
     'L2_xattn_bo2': (0.0, 0.1),
     'L2_xattn_g2': (1.0, 0.2),
     'L2_xattn_b2': (0.0, 0.1),
     'L2_xattn_bf1': (0.0, 0.352),
     'L2_xattn_bf2': (0.0, 0.1),
     'L2_xattn_g3': (1.0, 0.2),
     'L2_xattn_b3': (0.0, 0.1),
     'L3_xattn_bqkv': (0.0, 0.466),
     'L3_xattn_bos': (0.0, 0.1),
     'L3_xattn_bq': (0.0, 2.0),
     'L3_xattn_bkv': (0.0, 0.372),
     'L3_xattn_boc': (0.0, 0.1),
     'L3_xattn_b1': (0.0, 0.388),
     'L3_xattn_b2': (0.0, 0.1)}
    factors = {'L0_xattn_w_q': 2.715,
     'L2_xattn_Wqkv': 8.0,
     'L2_xattn_Wo1': 8.0,
     'L2_xattn_Wq': 8.0,
     'L2_xattn_Wk': 8.0,
     'L2_xattn_Wv': 8.0,
     'L2_xattn_Wo2': 8.0,
     'L3_xattn_Wq': 64.0}
    for name, (base, spread) in spreads.items():
        noise = np.random.default_rng([zlib.crc32(name.encode()), seed]).standard_normal(out[name].shape)
        drawn = base * np.exp(spread * noise) if base else spread * noise
        out[name] = jnp.asarray(drawn.astype(out[name].dtype))
    for name, factor in factors.items():
        out[name] = (out[name] * factor).astype(out[name].dtype)
    return out
```

```python
from contextlib import ExitStack

import numpy as np

import concourse.bass as bass
from concourse import mybir

F32 = mybir.dt.float32
BF16 = mybir.dt.bfloat16
I32 = mybir.dt.int32
ALU = mybir.AluOpType
ACT = mybir.ActivationFunctionType
AX_X = mybir.AxisListType.X

P = 128
SEQS, LEN, DIM = 128, 64, 128
HEADS, HD = 16, 8
HID = 512
PAIRS = SEQS * LEN // P
STREAMS = 2
ROUNDS = PAIRS // STREAMS
LAYERS = 7
PER_ROUND = LAYERS * STREAMS
QUADS, SLOTS = 4, 4
HALVES = 2
HCH = HID // P
SCALE = float(HD) ** -0.5
MASKED = -1e30

L0_SELF, L0_CROSS, L1_CROSS, L2_SELF, L2_CROSS, L3_SELF, L3_CROSS = range(LAYERS)
CROSS = {L0_CROSS, L1_CROSS, L2_CROSS, L3_CROSS}
PRE_NORM = {L0_SELF: 1e-5, L0_CROSS: 1e-5, L1_CROSS: 1e-6, L3_SELF: 1e-6, L3_CROSS: 1e-6}
POST_NORM = {L2_SELF: (0, 1e-5), L2_CROSS: (1, 1e-5)}
MLP = {L0_CROSS: 0, L2_CROSS: 1, L3_CROSS: 2}
MLP_PRE_NORM = {L0_CROSS: 1e-5, L3_CROSS: 1e-6}
MLP_POST_NORM = {L2_CROSS: (2, 1e-6)}
GELU = {L0_CROSS: ACT.Gelu, L2_CROSS: ACT.Gelu, L3_CROSS: ACT.Gelu_apprx_tanh}
Q_BIAS = {L0_SELF, L0_CROSS, L3_SELF, L3_CROSS}
K_BIAS = {L0_SELF, L3_SELF, L3_CROSS}
MASK = {L0_SELF: 0, L2_SELF: 1, L2_CROSS: 2}
ROW_SCALE = {L2_SELF: 0, L2_CROSS: 1}


def layer_of(j):
    return (j % PER_ROUND) // STREAMS


class Signal:

    def __init__(self, sem, per_layer):
        self.sem = sem
        self.per_layer = [per_layer.get(layer, 0) if isinstance(per_layer, dict) else per_layer
                          for layer in range(LAYERS)]
        self.round = STREAMS * sum(self.per_layer)

    def at(self, r, j, m=None):
        full, rest = divmod(j, PER_ROUND)
        before = full * self.round + sum(self.per_layer[layer_of(i)] for i in range(rest))
        return r * self.round + (before + (self.per_layer[layer_of(j)] if m is None else m))


def build(nc, a, out):
    ctx = ExitStack()
    with ctx:
        def sb(name, shape, dt=F32):
            return ctx.enter_context(nc.sbuf_tensor(name, shape, dt))

        def sem(name):
            return ctx.enter_context(nc.semaphore(name))

        def signal(name, per_layer=1):
            return Signal(sem(name), per_layer)

        ident = sb("ident", [P, P])
        ident_bf = sb("ident_bf", [P, P], BF16)
        slot_mask = sb("slot_mask", [P, SLOTS])
        causal = sb("causal", [P, LEN])
        rope_cos = sb("rope_cos", [P, LEN])
        rope_sin = sb("rope_sin", [P, LEN])
        w_q = sb("w_q", [P, LAYERS, DIM])
        w_k = sb("w_k", [P, LAYERS, DIM])
        w_v = sb("w_v", [P, LAYERS, DIM])
        w_o = sb("w_o", [P, LAYERS, DIM])
        w_q_rot = sb("w_q_rot", [P, DIM])
        w_k_rot = sb("w_k_rot", [P, DIM])
        w_1 = sb("w_1", [P, len(MLP), HID])
        w_2 = sb("w_2", [P, len(MLP), HCH, DIM])
        b_q = sb("b_q", [P, LAYERS])
        b_k = sb("b_k", [P, LAYERS])
        b_v = sb("b_v", [P, LAYERS])
        b_1 = sb("b_1", [P, len(MLP), HCH])
        b_o_rows = sb("b_o_rows", [P, LAYERS, DIM])
        b_2_rows = sb("b_2_rows", [P, len(MLP), DIM])
        post_g = sb("post_g", [P, 3, DIM])
        post_b = sb("post_b", [P, 3, DIM])
        mask_int = sb("mask_int", [P, LEN], I32)
        mask_f = sb("mask_f", [P, LEN])
        mask_bias = sb("mask_bias", [P, 3, LEN], BF16)
        row_scale = sb("row_scale", [P, 2])
        raw = sb("raw", [P, 20, DIM])
        raw_t = sb("raw_t", [P, 8, DIM])
        vecs = sb("vecs", [P, 8])
        b_v_wide = sb("b_v_wide", [P, 3, P])
        valid = sb("valid", [P, LEN])

        x_in = sb("x_in", [P, STREAMS, DIM])
        ctx_in = sb("ctx_in", [P, STREAMS, DIM])
        x = sb("x", [P, STREAMS, DIM])
        x_bias = sb("x_bias", [P, STREAMS, DIM])
        ctx_t = sb("ctx_t", [P, STREAMS, 2, 2, LEN])
        q_quads = sb("q_quads", [P, STREAMS, QUADS, P])
        k_slots = sb("k_slots", [P, STREAMS, SLOTS, P])
        v_ones = sb("v_ones", [P, STREAMS, 2, HEADS // 2, 32])
        row_max = sb("row_max", [P, HALVES, 8])
        scaled_max = sb("scaled_max", [P, HALVES, 8])
        shifted = sb("shifted", [P, HALVES, 512])
        probs = sb("probs", [P, HALVES, 4, P])
        pv_sb = sb("pv_sb", [P, HALVES, P])
        recip = sb("recip", [P, HEADS])
        attn = sb("attn", [P, DIM])
        attn_t = sb("attn_t", [P, P])
        stats = sb("stats", [P, 6])
        mean_var = sb("mean_var", [P, 2])
        mean_sq = sb("mean_sq", [P, 1])
        var_eps = sb("var_eps", [P, 1])
        rstd = sb("rstd", [P, 1])
        minus_half = sb("minus_half", [P, 1])
        normed = sb("normed", [P, DIM])
        h_t = sb("h_t", [P, 2, 2, LEN])
        mlp_h_t = sb("mlp_h_t", [P, P])
        gelu = sb("gelu", [P, HCH, P])
        rope_a = sb("rope_a", [P, 2, P])
        rope_b = sb("rope_b", [P, 2, P])
        rope_qk = sb("rope_qk", [P, 2, P])

        def bank(name):
            return ctx.enter_context(nc.psum_tensor(name, [P, 512], F32))

        ps_scores = [bank("ps_scores0"), bank("ps_scores1")]
        ps_scores_t = [bank("ps_scores_t0"), bank("ps_scores_t1")]
        ps_pv = bank("ps_pv")
        ps_dense = bank("ps_dense")
        ps_q = bank("ps_q")
        ps_k = bank("ps_k")

        consts_in = sem("consts_in")
        setup_mem = sem("setup_mem")
        setup_pe = sem("setup_pe")
        setup_dve = sem("setup_dve")
        first = {L0_SELF: 1}
        x_loaded = [signal(f"x_loaded{s}") for s in range(STREAMS)]
        ctx_loaded = [signal(f"ctx_loaded{s}") for s in range(STREAMS)]
        stored = [signal(f"stored{s}") for s in range(STREAMS)]
        scores_ready = signal("scores_ready", HALVES)
        scores_t_ready = signal("scores_t_ready", HALVES)
        pv_ready = signal("pv_ready")
        pv_t_ready = signal("pv_t_ready")
        attn_t_ready = signal("attn_t_ready")
        y_ready = signal("y_ready")
        mlp_t_ready = signal("mlp_t_ready", {n: 1 for n in MLP})
        hidden_ready = signal("hidden_ready", {n: 1 for n in MLP})
        mlp_y_ready = signal("mlp_y_ready", {n: 1 for n in MLP})
        h_t_ready = signal("h_t_ready")
        ctx_t_ready = signal("ctx_t_ready", first)
        q_ready = signal("q_ready")
        k_ready = signal("k_ready")
        v_ready = signal("v_ready")
        max_done = signal("max_done", {n: 4 if n in ROW_SCALE else 2 for n in range(LAYERS)})
        shifted_ready = signal("shifted_ready", HALVES)
        recip_done = signal("recip_done")
        attn_ready = signal("attn_ready")
        x_ready = signal("x_ready")
        post_steps = signal("post_steps", {n: 5 for n in POST_NORM})
        mlp_steps = signal("mlp_steps", {n: 2 for n in MLP_PRE_NORM})
        mlp_h_ready = signal("mlp_h_ready", {n: 1 for n in MLP_PRE_NORM})
        mlp_x_ready = signal("mlp_x_ready", {n: 1 for n in MLP})
        mlp_post_steps = signal("mlp_post_steps", {n: 5 for n in MLP_POST_NORM})
        pre_steps = signal("pre_steps", {n: 3 if n == L1_CROSS else 2 for n in PRE_NORM})
        h_ready = signal("h_ready", {n: 1 for n in PRE_NORM})
        rope_steps = signal("rope_steps", {L1_CROSS: 4})
        rope_ready = signal("rope_ready", {L1_CROSS: 1})
        k_slots_ready = signal("k_slots_ready")
        probs_ready = signal("probs_ready", HALVES)
        pv_copied = signal("pv_copied")
        attn_t_copied = signal("attn_t_copied")
        mlp_t_copied = signal("mlp_t_copied", {n: 1 for n in MLP})
        gelu_ready = signal("gelu_ready", {n: 1 for n in MLP})
        h_t_copied = signal("h_t_copied")
        ctx_t_copied = signal("ctx_t_copied", first)
        q_quads_ready = signal("q_quads_ready")
        v_ready_sb = signal("v_ready_sb")
        post_rstd = signal("post_rstd", {n: 1 for n in POST_NORM})
        mlp_rstd = signal("mlp_rstd", {n: 1 for n in MLP_PRE_NORM})
        mlp_post_rstd = signal("mlp_post_rstd", {n: 1 for n in MLP_POST_NORM})
        pre_rstd = signal("pre_rstd", {n: 1 for n in PRE_NORM})
        x_bias_ready = signal("x_bias_ready")
        mlp_x_bias_ready = signal("mlp_x_bias_ready", {n: 1 for n in MLP})

        x_dram = a["x"].rearrange("(n two) t c -> n (two t) c", two=2)
        ctx_dram = a["ctx_1024"].rearrange("(n two) t c -> n (two t) c", two=2)
        out_dram = out.rearrange("(n two) t c -> n (two t) c", two=2)

        def rounds(eng, pre, phase, post):
            pre(0, 0)
            phase(0, 0, with_post=False)
            with eng.Fori(0, ROUNDS - 1) as r:
                for j in range(1, PER_ROUND + 1):
                    phase(r, j)
            for j in range(1, PER_ROUND):
                phase(ROUNDS - 1, j, with_pre=j < PER_ROUND - 1)
            post(ROUNDS - 1, PER_ROUND - 1)

        def load_count(r, j):
            return r * 16 + (16 * (j // PER_ROUND) + 16)

        def first_round(r, j):
            return isinstance(r, int) and PER_ROUND * r + j < STREAMS

        def last_x_signal(layer):
            return mlp_x_ready if layer in MLP else x_ready

        def col(name, lo=0):
            return a[name][lo:lo + P].unsqueeze(1)

        def row(name):
            return a[name].unsqueeze(0).to_broadcast([P, DIM])

        def chunks(name, n):
            return a[name].rearrange("(n p) c -> p n c", p=P) if n > 1 else a[name]

        loads = [
            (ident[:, :], a["c_ident"]), (slot_mask[:, :], a["c_slot"]), (causal[:, :], a["c_causal"]),
            (rope_cos[:, :], a["c_cos"]), (rope_sin[:, :], a["c_sin"]),
            (raw[:, 0:3, :], chunks("L0_xattn_w_qkv", 3)), (raw[:, 3, :], a["L0_xattn_w_q"]),
            (raw[:, 4:8, :], chunks("L0_xattn_w_fc1", 4)), (raw[:, 8, :], a["L1_xattn_Wq"]),
            (raw[:, 9, :], a["L0_xattn_w_prj1"]), (raw[:, 10, :], a["L0_xattn_w_prj2"]),
            (raw[:, 11:13, :], chunks("L0_xattn_w_kv", 2)), (raw[:, 13:15, :], chunks("L1_xattn_Wkv", 2)),
            (raw[:, 15, :], a["L1_xattn_Wo"]),
            (raw[:, 16:20, :], a["L0_xattn_w_fc2"].rearrange("p (n c) -> p n c", c=P)),
            (vecs[:, 0:1], col("L0_xattn_ln1_g")), (vecs[:, 1:2], col("L0_xattn_ln1_b")),
            (vecs[:, 2:3], col("L0_xattn_ln2_g")), (vecs[:, 3:4], col("L0_xattn_ln2_b")),
            (vecs[:, 4:5], col("L0_xattn_ln3_g")), (vecs[:, 5:6], col("L0_xattn_ln3_b")),
            (vecs[:, 6:7], col("L1_xattn_norm_w")),
            (w_q[:, 3, :], a["L2_xattn_Wqkv"][:, 0:128]), (w_k[:, 3, :], a["L2_xattn_Wqkv"][:, 128:256]),
            (w_v[:, 3, :], a["L2_xattn_Wqkv"][:, 256:384]), (w_o[:, 3, :], a["L2_xattn_Wo1"]),
            (w_q[:, 4, :], a["L2_xattn_Wq"]), (w_k[:, 4, :], a["L2_xattn_Wk"]),
            (w_v[:, 4, :], a["L2_xattn_Wv"]), (w_o[:, 4, :], a["L2_xattn_Wo2"]),
            (w_q[:, 5, :], a["L3_xattn_Wqkv"][:, 0:128]), (w_k[:, 5, :], a["L3_xattn_Wqkv"][:, 128:256]),
            (w_v[:, 5, :], a["L3_xattn_Wqkv"][:, 256:384]), (w_o[:, 5, :], a["L3_xattn_Wos"]),
            (w_q[:, 6, :], a["L3_xattn_Wq"]), (w_k[:, 6, :], a["L3_xattn_Wkv"][:, 0:128]),
            (w_v[:, 6, :], a["L3_xattn_Wkv"][:, 128:256]), (w_o[:, 6, :], a["L3_xattn_Woc"]),
            (w_1[:, 1, :], a["L2_xattn_W1"]), (w_1[:, 2, :], a["L3_xattn_W1"]),
            (w_2[:, 1, :, :], chunks("L2_xattn_W2", 4)), (w_2[:, 2, :, :], chunks("L3_xattn_W2", 4)),
            (b_q[:, 5:6], col("L3_xattn_bqkv")), (b_k[:, 5:6], col("L3_xattn_bqkv", 128)),
            (b_v[:, 5:6], col("L3_xattn_bqkv", 256)), (b_q[:, 6:7], col("L3_xattn_bq")),
            (b_k[:, 6:7], col("L3_xattn_bkv")), (b_v[:, 6:7], col("L3_xattn_bkv", 128)),
            (b_o_rows[:, 0, :], row("L0_xattn_b_prj1")), (b_o_rows[:, 1, :], row("L0_xattn_b_prj2")),
            (b_o_rows[:, 3, :], row("L2_xattn_bo1")), (b_o_rows[:, 4, :], row("L2_xattn_bo2")),
            (b_o_rows[:, 5, :], row("L3_xattn_bos")), (b_o_rows[:, 6, :], row("L3_xattn_boc")),
            (b_2_rows[:, 0, :], row("L0_xattn_b_fc2")), (b_2_rows[:, 1, :], row("L2_xattn_bf2")),
            (b_2_rows[:, 2, :], row("L3_xattn_b2")),
            (post_g[:, 0, :], row("L2_xattn_g1")), (post_g[:, 1, :], row("L2_xattn_g2")),
            (post_g[:, 2, :], row("L2_xattn_g3")), (post_b[:, 0, :], row("L2_xattn_b1")),
            (post_b[:, 1, :], row("L2_xattn_b2")), (post_b[:, 2, :], row("L2_xattn_b3")),
            (mask_int[:, :], a["mask_1xS2_if1"].to_broadcast([P, LEN])),
        ]
        for m, name in enumerate(("L0_xattn_b_fc1", "L2_xattn_bf1", "L3_xattn_b1")):
            for c in range(HCH):
                loads.append((b_1[:, m, c:c + 1], col(name, c * P)))
        N_LOADS = len(loads)
        scaled_to = [(w_q[:, 0, :], 0), (w_k[:, 0, :], 0), (w_v[:, 0, :], 0), (w_q[:, 1, :], 2)] + \
                    [(w_1[:, 0, c * P:(c + 1) * P], 4) for c in range(HCH)] + [(w_q[:, 2, :], 6)]
        copied_to = [w_o[:, 0, :], w_o[:, 1, :], w_k[:, 1, :], w_v[:, 1, :], w_k[:, 2, :], w_v[:, 2, :],
                     w_o[:, 2, :]] + [w_2[:, 0, c, :] for c in range(HCH)]
        setup_banks = [ps_scores[0], ps_scores[1], ps_scores_t[0], ps_scores_t[1], ps_pv]

        def setup_psum(n):
            return setup_banks[n // 4][:, (n % 4) * P:(n % 4 + 1) * P]

        N_MEM = 8
        STORED_0 = 1

        with nc.Block() as block:

            @block.sync
            def _(sp):
                for dst, src in loads[0::2]:
                    sp.dma_start(dst, src).then_inc(consts_in, 16)

                def load(n, s):
                    sp.dma_start(x_in[:, s, :], x_dram[bass.ds(n, 1), :, :].rearrange("n p c -> (n p) c")
                                 if not isinstance(n, int) else x_dram[n]).then_inc(x_loaded[s].sem, 16)
                    sp.dma_start(ctx_in[:, s, :], ctx_dram[bass.ds(n, 1), :, :].rearrange("n p c -> (n p) c")
                                 if not isinstance(n, int) else ctx_dram[n]).then_inc(ctx_loaded[s].sem, 16)

                def store(r, n, s):
                    sp.wait_ge(mlp_x_ready.sem, mlp_x_ready.at(r, PER_ROUND - STREAMS + s))
                    sp.dma_start(out_dram[bass.ds(n, 1), :, :].rearrange("n p c -> (n p) c")
                                 if not isinstance(n, int) else out_dram[n], x[:, s, :]).then_inc(stored[s].sem, 16)

                for s in range(STREAMS):
                    load(s, s)
                with sp.Fori(0, ROUNDS - 1) as r:
                    pair = [sp.snap(STREAMS * r + k) for k in range(2 * STREAMS)]
                    sp.wait_ge(h_ready.sem, h_ready.at(r, STREAMS - 1))
                    sp.wait_ge(x_bias_ready.sem, x_bias_ready.at(r, STREAMS - 1))
                    sp.wait_ge(ctx_t_ready.sem, ctx_t_ready.at(r, STREAMS - 1))
                    for s in range(STREAMS):
                        load(pair[STREAMS + s], s)
                    for s in range(STREAMS):
                        store(r, pair[s], s)
                for s in range(STREAMS):
                    store(ROUNDS - 1, PAIRS - STREAMS + s, s)
                for s in range(STREAMS):
                    sp.wait_ge(stored[s].sem, 16 * ROUNDS + STORED_0)

            @block.gpsimd
            def _(pool):
                pool.memset(q_quads[:, :, :, :], 0.0).then_inc(setup_mem, 1)
                pool.memset(v_ones[:, :, :, :, 0:16], 0.0).then_inc(setup_mem, 1)
                pool.memset(b_o_rows[:, L1_CROSS, :], 0.0).then_inc(setup_mem, 1)
                pool.memset(minus_half[:, :], -0.5).then_inc(setup_mem, 1)
                pool.wait_ge(consts_in, 16 * N_LOADS)
                pool.wait_ge(setup_dve, SETUP_DVE)

                def inverse_root(r, j, steps, m, ready):
                    pool.wait_ge(steps.sem, steps.at(r, j, m))
                    pool.tensor_tensor(rstd[:, :], var_eps[:, :], minus_half[:, :],
                                       ALU.pow).then_inc(ready.sem, 1)

                def pre(r, j):
                    layer, s = layer_of(j), j % STREAMS
                    if layer in PRE_NORM:
                        inverse_root(r, j, pre_steps, None, pre_rstd)
                    if layer == L0_SELF:
                        pool.wait_ge(x_loaded[s].sem, load_count(r, j))
                        src = x_in
                        if not first_round(r, j):
                            pool.wait_ge(mlp_x_ready.sem, mlp_x_ready.at(r, j - STREAMS))
                    else:
                        done = last_x_signal(layer_of(j - STREAMS))
                        pool.wait_ge(done.sem, done.at(r, j - STREAMS))
                        src = x
                    pool.tensor_tensor(x_bias[:, s, :], src[:, s, :], b_o_rows[:, layer, :],
                                       ALU.add).then_inc(x_bias_ready.sem, 1)

                def post(r, j):
                    layer, s = layer_of(j), j % STREAMS
                    if layer in POST_NORM:
                        inverse_root(r, j, post_steps, 3, post_rstd)
                    if layer in MLP_PRE_NORM:
                        inverse_root(r, j, mlp_steps, None, mlp_rstd)
                    if layer in MLP:
                        pool.wait_ge(x_ready.sem, x_ready.at(r, j))
                        pool.tensor_tensor(x_bias[:, s, :], x[:, s, :], b_2_rows[:, MLP[layer], :],
                                           ALU.add).then_inc(mlp_x_bias_ready.sem, 1)
                    if layer in MLP_POST_NORM:
                        inverse_root(r, j, mlp_post_steps, 3, mlp_post_rstd)

                def phase(r, j, with_post=True, with_pre=True):
                    if with_post:
                        post(r, j - 1)
                    if with_pre:
                        pre(r, j + 1)

                rounds(pool, pre, phase, post)

            @block.scalar
            def _(act):
                for dst, src in loads[1::2]:
                    act.dma_start(dst, src).then_inc(consts_in, 16)
                act.wait_ge(consts_in, 16 * N_LOADS)
                act.wait_ge(setup_mem, N_MEM)
                act.wait_ge(setup_dve, SETUP_DVE)

                def copy_h_t(r, j):
                    act.wait_ge(h_t_ready.sem, h_t_ready.at(r, j))
                    nc.scalar.copy(h_t[:, :, :, :], ps_dense[:, 0:P].rearrange("p (b t) -> p b t", b=2)
                                   .unsqueeze(2).to_broadcast([P, 2, 2, LEN])).then_inc(h_t_copied.sem, 1)

                def pre(r, j):
                    layer, s = layer_of(j), j % STREAMS
                    copy_h_t(r, j)
                    if layer == L0_SELF:
                        act.wait_ge(ctx_t_ready.sem, ctx_t_ready.at(r, j))
                        nc.scalar.copy(ctx_t[:, s, :, :, :], ps_dense[:, P:2 * P]
                                       .rearrange("p (b t) -> p b t", b=2).unsqueeze(2)
                                       .to_broadcast([P, 2, 2, LEN])).then_inc(ctx_t_copied.sem, 1)
                    if layer == L1_CROSS:
                        act.wait_ge(rope_ready.sem, rope_ready.at(r, j))
                        src = rope_qk[:, 0, :]
                    else:
                        act.wait_ge(q_ready.sem, q_ready.at(r, j))
                        src = ps_q[:, 0:P]
                    for g in range(QUADS):
                        rows = slice(32 * g, 32 * g + 32)
                        if layer in Q_BIAS:
                            ins = nc.scalar.activation(q_quads[rows, s, g, :], src[rows, :], ACT.Identity,
                                                       bias=b_q[rows, layer:layer + 1])
                        else:
                            ins = nc.scalar.copy(q_quads[rows, s, g, :], src[rows, :])
                    ins.then_inc(q_quads_ready.sem, 1)
                    act.wait_ge(v_ready.sem, v_ready.at(r, j))
                    for e in range(2):
                        rows = slice(64 * e, 64 * e + 64)
                        ins = nc.scalar.copy(
                            v_ones[rows, s, :, :, HD * e:HD * e + HD].rearrange("p b h d -> p (b h) d"),
                            ps_dense[rows, 256:512].rearrange("p (bh e d) -> p bh e d", e=2, d=HD)[:, :, e, :])
                    ins.then_inc(v_ready_sb.sem, 1)

                def copy_pv(r, j):
                    act.wait_ge(pv_ready.sem, pv_ready.at(r, j))
                    nc.scalar.copy(pv_sb[:, :, :], ps_pv[:, 0:256].rearrange("p (u t) -> p u t", u=2)) \
                        .then_inc(pv_copied.sem, 1)

                def copy_attn_t(r, j):
                    act.wait_ge(attn_t_ready.sem, attn_t_ready.at(r, j))
                    nc.scalar.copy(attn_t[:, :], ps_dense[:, 256:384]).then_inc(attn_t_copied.sem, 1)

                def mlp(r, j):
                    layer = layer_of(j)
                    if layer not in MLP:
                        return
                    act.wait_ge(mlp_t_ready.sem, mlp_t_ready.at(r, j))
                    nc.scalar.copy(mlp_h_t[:, :], ps_dense[:, 0:P]).then_inc(mlp_t_copied.sem, 1)
                    act.wait_ge(hidden_ready.sem, hidden_ready.at(r, j))
                    for c in range(HCH):
                        ins = nc.scalar.activation(gelu[:, c, :], ps_q[:, c * P:(c + 1) * P], GELU[layer],
                                                   bias=b_1[:, MLP[layer], c:c + 1])
                    ins.then_inc(gelu_ready.sem, 1)

                def exps(r, j, u):
                    act.wait_ge(scores_t_ready.sem, scores_t_ready.at(r, j, u + 1))
                    nc.scalar.activation(probs[:, u, :, :], ps_scores_t[u][:, :]
                                         .rearrange("p (h t) -> p h t", h=4), ACT.Exp,
                                         scale=SCALE).then_inc(probs_ready.sem, 1)

                def post(r, j):
                    copy_pv(r, j)
                    copy_attn_t(r, j)
                    mlp(r, j)

                def phase(r, j, with_post=True, with_pre=True):
                    if with_post:
                        copy_pv(r, j - 1)
                        copy_attn_t(r, j - 1)
                    exps(r, j, 0)
                    exps(r, j, 1)
                    if with_post:
                        mlp(r, j - 1)
                    if with_pre:
                        pre(r, j + 1)

                rounds(act, pre, phase, post)

            @block.tensor
            def _(pe):
                pe.wait_ge(consts_in, 16 * N_LOADS)
                pe.wait_ge(setup_mem, N_MEM)
                for n in range(20):
                    ins = nc.tensor.transpose(setup_psum(n), raw[:, n, :], ident[:, :])
                ins.then_inc(setup_pe, 1)
                pe.wait_ge(setup_dve, SETUP_RAW_T)
                for i, (n, vec) in enumerate(((0, 1), (1, 1), (2, 1), (3, 3), (4, 5), (5, 5), (6, 5), (7, 5))):
                    ins = nc.tensor.matmul(ps_q[:, i:i + 1], raw_t[:, n, :], vecs[:, vec:vec + 1],
                                           start=True, stop=True)
                ins.then_inc(setup_pe, 1)
                pe.wait_ge(setup_dve, SETUP_WIDE)
                for i, layer in enumerate((0, 5, 6)):
                    ins = nc.tensor.matmul(ps_k[:, i * P:(i + 1) * P], b_v_wide[:, i, :], w_o[:, layer, :],
                                           start=True, stop=True)
                ins.then_inc(setup_pe, 1)
                pe.wait_ge(setup_dve, SETUP_DVE)

                def pre_h(r, j):
                    layer, s = layer_of(j), j % STREAMS
                    if layer in PRE_NORM:
                        pe.wait_ge(h_ready.sem, h_ready.at(r, j))
                        src = normed[:, :]
                        if layer == L0_SELF and not first_round(r, j):
                            pe.wait_ge(mlp_x_ready.sem, mlp_x_ready.at(r, j - STREAMS))
                    else:
                        done = last_x_signal(layer_of(j - STREAMS))
                        pe.wait_ge(done.sem, done.at(r, j - STREAMS))
                        src = x[:, s, :]
                    nc.tensor.transpose(ps_dense[:, 0:P], src, ident[:, :]).then_inc(h_t_ready.sem, 1)
                    if layer == L0_SELF:
                        pe.wait_ge(ctx_loaded[s].sem, load_count(r, j))
                        pe.wait_ge(h_t_copied.sem, h_t_copied.at(r, j))
                        nc.tensor.transpose(ps_dense[:, P:2 * P], ctx_in[:, s, :], ident[:, :]) \
                            .then_inc(ctx_t_ready.sem, 1)

                def pre_qk(r, j):
                    layer, s = layer_of(j), j % STREAMS
                    pe.wait_ge(h_t_copied.sem, h_t_copied.at(r, j))
                    tokens = h_t[:, :, 0, :]
                    kv_tokens = ctx_t[:, s, :, 0, :] if layer in CROSS else tokens
                    ins = nc.tensor.matmul(ps_q[:, 0:P], w_q[:, layer, :], tokens, start=True, stop=True)
                    if layer == L1_CROSS:
                        ins = nc.tensor.matmul(ps_q[:, P:2 * P], w_q_rot[:, :], tokens, start=True, stop=True)
                    ins.then_inc(q_ready.sem, 1)
                    ins = nc.tensor.matmul(ps_k[:, 0:P], w_k[:, layer, :], kv_tokens, start=True, stop=True)
                    if layer == L1_CROSS:
                        ins = nc.tensor.matmul(ps_k[:, P:2 * P], w_k_rot[:, :], kv_tokens, start=True, stop=True)
                    ins.then_inc(k_ready.sem, 1)

                def pre_v(r, j):
                    layer, s = layer_of(j), j % STREAMS
                    if layer == L0_SELF:
                        pe.wait_ge(ctx_t_copied.sem, ctx_t_copied.at(r, j))
                    for b in range(2):
                        src = ctx_t[:, s, b, :, :] if layer in CROSS else h_t[:, b, :, :]
                        ins = nc.tensor.matmul(ps_dense[:, 256 + b * P:256 + (b + 1) * P],
                                               src.rearrange("p k t -> p (k t)"), w_v[:, layer, :],
                                               start=True, stop=True)
                    ins.then_inc(v_ready.sem, 1)

                def pre(r, j):
                    pre_h(r, j)
                    pre_qk(r, j)
                    pre_v(r, j)

                def scores(r, j, u):
                    layer, s = layer_of(j), j % STREAMS
                    if u == 0:
                        pe.wait_ge(q_quads_ready.sem, q_quads_ready.at(r, j))
                        pe.wait_ge(k_slots_ready.sem, k_slots_ready.at(r, j))
                    for g in (2 * u, 2 * u + 1):
                        cols = slice((g % 2) * 256, (g % 2) * 256 + 256)
                        for b in range(2):
                            ins = nc.tensor.matmul(ps_scores[u][64 * b:64 * b + 64, cols],
                                                   q_quads[:, s, g, 64 * b:64 * b + 64],
                                                   k_slots[:, s, :, 64 * b:64 * b + 64],
                                                   start=True, stop=layer not in MASK)
                        if layer in MASK:
                            for b in range(2):
                                ins = nc.tensor.matmul(ps_scores[u][64 * b:64 * b + 64, cols],
                                                       ident_bf[:, 64 * b:64 * b + 64],
                                                       mask_bias[:, MASK[layer], :].unsqueeze(1)
                                                       .to_broadcast([P, SLOTS, LEN]),
                                                       start=False, stop=True)
                    ins.then_inc(scores_ready.sem, 1)

                def transposes(r, j, u):
                    pe.wait_ge(shifted_ready.sem, shifted_ready.at(r, j, u + 1))
                    for h in range(4):
                        ins = nc.tensor.transpose(ps_scores_t[u][:, h * P:(h + 1) * P],
                                                  shifted[:, u, h * P:(h + 1) * P], ident[:, :])
                    ins.then_inc(scores_t_ready.sem, 1)

                def values(r, j, u):
                    s = j % STREAMS
                    if u == 0:
                        pe.wait_ge(v_ready_sb.sem, v_ready_sb.at(r, j))
                    pe.wait_ge(probs_ready.sem, probs_ready.at(r, j, u + 1))
                    for b in range(2):
                        for h in range(4):
                            ins = nc.tensor.matmul(ps_pv[32 * h:32 * h + 32, u * P + 64 * b:u * P + 64 * b + 64],
                                                   v_ones[:, s, b, 4 * u + h, :],
                                                   probs[:, u, h, 64 * b:64 * b + 64], start=True, stop=True)
                    if u == HALVES - 1:
                        ins.then_inc(pv_ready.sem, 1)

                def pv_t(r, j):
                    pe.wait_ge(pv_copied.sem, pv_copied.at(r, j))
                    for u in range(HALVES):
                        ins = nc.tensor.transpose(ps_dense[:, u * P:(u + 1) * P], pv_sb[:, u, :], ident[:, :])
                    ins.then_inc(pv_t_ready.sem, 1)

                def attn_turn(r, j):
                    pe.wait_ge(attn_ready.sem, attn_ready.at(r, j))
                    nc.tensor.transpose(ps_dense[:, 256:384], attn[:, :], ident[:, :]) \
                        .then_inc(attn_t_ready.sem, 1)

                def project(r, j):
                    pe.wait_ge(attn_t_copied.sem, attn_t_copied.at(r, j))
                    nc.tensor.matmul(ps_dense[:, 384:512], attn_t[:, :], w_o[:, layer_of(j), :],
                                     start=True, stop=True).then_inc(y_ready.sem, 1)

                def mlp_up(r, j):
                    layer, s = layer_of(j), j % STREAMS
                    if layer not in MLP:
                        return
                    if layer in MLP_PRE_NORM:
                        pe.wait_ge(mlp_h_ready.sem, mlp_h_ready.at(r, j))
                        src = normed[:, :]
                    else:
                        pe.wait_ge(x_ready.sem, x_ready.at(r, j))
                        src = x[:, s, :]
                    nc.tensor.transpose(ps_dense[:, 0:P], src, ident[:, :]).then_inc(mlp_t_ready.sem, 1)
                    pe.wait_ge(mlp_t_copied.sem, mlp_t_copied.at(r, j))
                    for c in range(HCH):
                        ins = nc.tensor.matmul(ps_q[:, c * P:(c + 1) * P],
                                               w_1[:, MLP[layer], c * P:(c + 1) * P], mlp_h_t[:, :],
                                               start=True, stop=True)
                    ins.then_inc(hidden_ready.sem, 1)

                def mlp_down(r, j):
                    layer = layer_of(j)
                    if layer not in MLP:
                        return
                    pe.wait_ge(gelu_ready.sem, gelu_ready.at(r, j))
                    for c in range(HCH):
                        ins = nc.tensor.matmul(ps_dense[:, P:2 * P], gelu[:, c, :], w_2[:, MLP[layer], c, :],
                                               start=c == 0, stop=c == HCH - 1)
                    ins.then_inc(mlp_y_ready.sem, 1)

                def post(r, j):
                    pe.wait_ge(mlp_x_ready.sem, mlp_x_ready.at(r, j - 1))
                    pv_t(r, j)
                    attn_turn(r, j)
                    project(r, j)
                    mlp_up(r, j)
                    mlp_down(r, j)

                def phase(r, j, with_post=True, with_pre=True):
                    scores(r, j, 0)
                    if with_post:
                        pv_t(r, j - 1)
                    scores(r, j, 1)
                    if with_post:
                        attn_turn(r, j - 1)
                    transposes(r, j, 0)
                    if with_post:
                        project(r, j - 1)
                    transposes(r, j, 1)
                    values(r, j, 0)
                    if with_post:
                        mlp_up(r, j - 1)
                        if layer_of(j - 1) in MLP:
                            values(r, j, 1)
                        mlp_down(r, j - 1)
                    if with_pre:
                        pre_h(r, j + 1)
                        pre_qk(r, j + 1)
                    if not (with_post and layer_of(j - 1) in MLP):
                        values(r, j, 1)
                    if with_pre:
                        pre_v(r, j + 1)

                rounds(pe, pre, phase, post)

            @block.vector
            def _(dve):
                v = nc.vector
                for rows, one, zero in ((slice(0, 64), 16, 24), (slice(64, 128), 24, 16)):
                    v.memset(v_ones[rows, :, :, :, one:one + HD], 1.0).then_inc(setup_mem, 1)
                    v.memset(v_ones[rows, :, :, :, zero:zero + HD], 0.0).then_inc(setup_mem, 1)
                dve.wait_ge(consts_in, 16 * N_LOADS)
                dve.wait_ge(setup_mem, N_MEM)
                for s in range(STREAMS):
                    v.memset(scaled_max[:, s, :], 0.0).then_inc(stored[s].sem, STORED_0)
                done = [0]

                def step(ins):
                    done[0] += 1
                    ins.then_inc(setup_dve, 1)
                    dve.wait_ge(setup_dve, done[0])

                dve.wait_ge(setup_pe, 1)
                for n in range(8):
                    step(v.tensor_copy(raw_t[:, n, :], setup_psum(n)))
                assert done[0] == SETUP_RAW_T
                for n, (dst, vec) in enumerate(scaled_to):
                    step(v.tensor_scalar(dst, setup_psum(n), vecs[:, vec:vec + 1], None, ALU.mult))
                for n, dst in enumerate(copied_to):
                    step(v.tensor_copy(dst, setup_psum(len(scaled_to) + n)))
                dve.wait_ge(setup_pe, 2)
                step(v.tensor_copy(b_q[:, 0:1], ps_q[:, 0:1]))
                step(v.tensor_copy(b_k[:, 0:1], ps_q[:, 1:2]))
                step(v.tensor_copy(b_v[:, 0:1], ps_q[:, 2:3]))
                step(v.tensor_copy(b_q[:, 1:2], ps_q[:, 3:4]))
                step(v.tensor_tensor(b_1[:, 0, :], ps_q[:, 4:8], b_1[:, 0, :], ALU.add))
                for i, layer in enumerate((0, 5, 6)):
                    step(v.tensor_copy(b_v_wide[:, i, :], b_v[:, layer:layer + 1].to_broadcast([P, P])))
                assert done[0] == SETUP_WIDE
                for w, w_rot in ((w_q, w_q_rot), (w_k, w_k_rot)):
                    src = w[:, L1_CROSS, :].rearrange("p (h a d) -> p h a d", a=2, d=HD // 2)
                    dst = w_rot[:, :].rearrange("p (h a d) -> p h a d", a=2, d=HD // 2)
                    step(v.tensor_scalar(dst[:, :, 0, :], src[:, :, 1, :], -1.0, None, ALU.mult))
                    step(v.tensor_copy(dst[:, :, 1, :], src[:, :, 0, :]))
                step(v.tensor_copy(ident_bf[:, :], ident[:, :]))
                step(v.tensor_copy(mask_f[:, :], mask_int[:, :]))
                step(v.tensor_scalar(mask_bias[:, 0, :], causal[:, :], -1.0, -MASKED, ALU.add, ALU.mult))
                step(v.tensor_tensor(valid[:, :], causal[:, :], mask_f[:, :], ALU.mult))
                for i, src in enumerate((valid, mask_f)):
                    step(v.tensor_reduce(row_scale[:, i:i + 1], src[:, :], AX_X, ALU.max))
                    step(v.tensor_scalar(src[:, :], src[:, :], -1.0, -MASKED, ALU.add, ALU.mult))
                    step(v.tensor_scalar(mask_bias[:, 1 + i, :], src[:, :], row_scale[:, i:i + 1], None,
                                         ALU.mult))
                dve.wait_ge(setup_pe, 3)
                for i, layer in enumerate((0, 5, 6)):
                    step(v.tensor_tensor(b_o_rows[:, layer, :], ps_k[:, i * P:(i + 1) * P],
                                         b_o_rows[:, layer, :], ALU.add))
                assert done[0] == SETUP_DVE, done[0]

                def norm_factors(r, j, src, steps, rstd_ready, eps, at=0, rms=False):
                    v.bn_stats(stats[:, :], src)
                    dve.drain()
                    v.bn_aggr(mean_var[:, :], stats[:, :]).then_inc(steps.sem, 1)
                    dve.wait_ge(steps.sem, steps.at(r, j, at + 1))
                    var = mean_var[:, 1:2]
                    if rms:
                        v.scalar_tensor_tensor(out=mean_sq[:, :], in0=mean_var[:, 0:1], scalar=mean_var[:, 0:1],
                                               in1=var, op0=ALU.mult, op1=ALU.add).then_inc(steps.sem, 1)
                        dve.wait_ge(steps.sem, steps.at(r, j, at + 2))
                        var = mean_sq[:, :]
                    v.tensor_scalar(var_eps[:, :], var, eps, None, ALU.add).then_inc(steps.sem, 1)
                    dve.wait_ge(rstd_ready.sem, rstd_ready.at(r, j))

                def post_norm(r, j, steps, rstd_ready, which, ready):
                    s = j % STREAMS
                    g, eps = which
                    dve.wait_ge(steps.sem, steps.at(r, j, 1))
                    norm_factors(r, j, x[:, s, :], steps, rstd_ready, eps, at=1)
                    v.tensor_scalar(normed[:, :], x[:, s, :], mean_var[:, 0:1], rstd[:, 0:1],
                                    ALU.subtract, ALU.mult).then_inc(steps.sem, 1)
                    dve.wait_ge(steps.sem, steps.at(r, j, 4))
                    v.tensor_tensor(normed[:, :], normed[:, :], post_g[:, g, :], ALU.mult).then_inc(steps.sem, 1)
                    dve.wait_ge(steps.sem, steps.at(r, j, 5))
                    v.tensor_tensor(x[:, s, :], normed[:, :], post_b[:, g, :], ALU.add).then_inc(ready.sem, 1)

                def pre_norm(r, j):
                    layer, s = layer_of(j), j % STREAMS
                    if layer not in PRE_NORM:
                        return
                    if layer == L0_SELF:
                        dve.wait_ge(x_loaded[s].sem, load_count(r, j))
                        src = x_in[:, s, :]
                    else:
                        before = last_x_signal(layer_of(j - STREAMS))
                        dve.wait_ge(before.sem, before.at(r, j - STREAMS))
                        src = x[:, s, :]
                    norm_factors(r, j, src, pre_steps, pre_rstd, PRE_NORM[layer], rms=layer == L1_CROSS)
                    if layer == L1_CROSS:
                        ins = v.tensor_scalar(normed[:, :], src, rstd[:, 0:1], None, ALU.mult)
                    else:
                        ins = v.tensor_scalar(normed[:, :], src, mean_var[:, 0:1], rstd[:, 0:1],
                                              ALU.subtract, ALU.mult)
                    ins.then_inc(h_ready.sem, 1)

                def pre_k(r, j):
                    layer, s = layer_of(j), j % STREAMS
                    mask = slot_mask[:, :].unsqueeze(2).to_broadcast([P, SLOTS, P])
                    dve.wait_ge(k_ready.sem, k_ready.at(r, j))
                    src = ps_k[:, 0:P]
                    if layer == L1_CROSS:
                        dve.wait_ge(q_ready.sem, q_ready.at(r, j))
                        cos = rope_cos[:, :].unsqueeze(1).to_broadcast([P, 2, LEN])
                        sin = rope_sin[:, :].unsqueeze(1).to_broadcast([P, 2, LEN])

                        def two(t):
                            return t.rearrange("p (b t) -> p b t", b=2)

                        for i, ps in enumerate((ps_q, ps_k)):
                            v.tensor_tensor(two(rope_a[:, i, :]), two(ps[:, 0:P]), cos,
                                            ALU.mult).then_inc(rope_steps.sem, 1)
                            v.tensor_tensor(two(rope_b[:, i, :]), two(ps[:, P:2 * P]), sin,
                                            ALU.mult).then_inc(rope_steps.sem, 1)
                        dve.wait_ge(rope_steps.sem, rope_steps.at(r, j))
                        v.tensor_tensor(rope_qk[:, :, :], rope_a[:, :, :], rope_b[:, :, :],
                                        ALU.add).then_inc(rope_ready.sem, 1)
                        dve.wait_ge(rope_ready.sem, rope_ready.at(r, j))
                        src = rope_qk[:, 1, :]
                    src = src.unsqueeze(1).to_broadcast([P, SLOTS, P])
                    if layer in K_BIAS:
                        ins = v.scalar_tensor_tensor(out=k_slots[:, s, :, :], in0=src,
                                                     scalar=b_k[:, layer:layer + 1], in1=mask,
                                                     op0=ALU.add, op1=ALU.mult)
                    else:
                        ins = v.tensor_tensor(k_slots[:, s, :, :], src, mask, ALU.mult)
                    ins.then_inc(k_slots_ready.sem, 1)

                def pre(r, j):
                    pre_norm(r, j)
                    pre_k(r, j)

                def shift(r, j, u):
                    layer = layer_of(j)
                    per_half = 2 if layer in ROW_SCALE else 1
                    heads = ps_scores[u][:, :].rearrange("p (h k) -> p h k", k=LEN)
                    dst = shifted[:, u, :].rearrange("p (h k) -> p h k", k=LEN)
                    dve.wait_ge(scores_ready.sem, scores_ready.at(r, j, u + 1))
                    v.tensor_reduce(row_max[:, u, :], heads, AX_X, ALU.max).then_inc(max_done.sem, 1)
                    dve.wait_ge(max_done.sem, max_done.at(r, j, per_half * u + 1))
                    if layer in ROW_SCALE:
                        scale = row_scale[:, ROW_SCALE[layer]:ROW_SCALE[layer] + 1]
                        v.tensor_scalar(scaled_max[:, u, :], row_max[:, u, :], scale, None,
                                        ALU.mult).then_inc(max_done.sem, 1)
                        dve.wait_ge(max_done.sem, max_done.at(r, j, per_half * u + 2))
                        ins = v.scalar_tensor_tensor(
                            out=dst, in0=heads, scalar=scale,
                            in1=scaled_max[:, u, :].unsqueeze(2).to_broadcast([P, 8, LEN]),
                            op0=ALU.mult, op1=ALU.subtract)
                    else:
                        ins = v.tensor_tensor(dst, heads, row_max[:, u, :].unsqueeze(2)
                                              .to_broadcast([P, 8, LEN]), ALU.subtract)
                    ins.then_inc(shifted_ready.sem, 1)

                def normalise(r, j):
                    dve.wait_ge(pv_t_ready.sem, pv_t_ready.at(r, j))
                    view = ps_dense[:, 0:256].rearrange("p (h w e d) -> p h w e d", w=2, e=2, d=HD)
                    v.reciprocal(recip[:, :].rearrange("p (h e) -> p h e", e=2),
                                 view[:, :, 1, :, 0]).then_inc(recip_done.sem, 1)
                    dve.wait_ge(recip_done.sem, recip_done.at(r, j))
                    v.tensor_tensor(attn[:, :].rearrange("p (h e d) -> p h e d", e=2, d=HD), view[:, :, 0, :, :],
                                    recip[:, :].rearrange("p (h e) -> p h e", e=2).unsqueeze(3)
                                    .to_broadcast([P, HEADS // 2, 2, HD]), ALU.mult).then_inc(attn_ready.sem, 1)

                def residual(r, j):
                    layer, s = layer_of(j), j % STREAMS
                    dve.wait_ge(y_ready.sem, y_ready.at(r, j))
                    dve.wait_ge(x_bias_ready.sem, x_bias_ready.at(r, j))
                    if layer == L0_SELF:
                        dve.wait_ge(stored[s].sem, r * 16 + 16 * (j // PER_ROUND) + STORED_0)
                    after = post_steps if layer in POST_NORM else x_ready
                    v.tensor_tensor(x[:, s, :], ps_dense[:, 384:512], x_bias[:, s, :],
                                    ALU.add).then_inc(after.sem, 1)
                    if layer in POST_NORM:
                        post_norm(r, j, post_steps, post_rstd, POST_NORM[layer], x_ready)

                def mlp_norm(r, j):
                    layer, s = layer_of(j), j % STREAMS
                    if layer not in MLP_PRE_NORM:
                        return
                    dve.wait_ge(x_ready.sem, x_ready.at(r, j))
                    norm_factors(r, j, x[:, s, :], mlp_steps, mlp_rstd, MLP_PRE_NORM[layer])
                    v.tensor_scalar(normed[:, :], x[:, s, :], mean_var[:, 0:1], rstd[:, 0:1],
                                    ALU.subtract, ALU.mult).then_inc(mlp_h_ready.sem, 1)

                def mlp_residual(r, j):
                    layer, s = layer_of(j), j % STREAMS
                    if layer not in MLP:
                        return
                    dve.wait_ge(mlp_y_ready.sem, mlp_y_ready.at(r, j))
                    dve.wait_ge(mlp_x_bias_ready.sem, mlp_x_bias_ready.at(r, j))
                    after = mlp_post_steps if layer in MLP_POST_NORM else mlp_x_ready
                    v.tensor_tensor(x[:, s, :], ps_dense[:, P:2 * P], x_bias[:, s, :],
                                    ALU.add).then_inc(after.sem, 1)
                    if layer in MLP_POST_NORM:
                        post_norm(r, j, mlp_post_steps, mlp_post_rstd, MLP_POST_NORM[layer], mlp_x_ready)

                def post(r, j):
                    normalise(r, j)
                    residual(r, j)
                    mlp_norm(r, j)
                    mlp_residual(r, j)

                def phase(r, j, with_post=True, with_pre=True):
                    shift(r, j, 0)
                    if with_post:
                        normalise(r, j - 1)
                    shift(r, j, 1)
                    if with_post:
                        residual(r, j - 1)
                        mlp_norm(r, j - 1)
                        mlp_residual(r, j - 1)
                    if with_pre:
                        pre(r, j + 1)

                rounds(dve, pre, phase, post)


SETUP_RAW_T = 8
SETUP_WIDE = SETUP_RAW_T + 9 + 11 + 5 + 3
SETUP_DVE = SETUP_WIDE + 4 + 4 + 6 + 3


def constants():
    c = np.arange(P)
    half = HD // 2
    inv_freq = (np.float32(1.0) / np.float32(10000.0) ** (np.arange(half, dtype=np.float32) / np.float32(half))).astype(np.float32)
    angle = (np.arange(LEN, dtype=np.float32)[None, :] * inv_freq[(c % half)][:, None]).astype(np.float32)
    return {
        "c_ident": np.eye(P, dtype=np.float32),
        "c_slot": ((c[:, None] // HD) % SLOTS == np.arange(SLOTS)[None, :]).astype(np.float32),
        "c_causal": ((c[:, None] % LEN) >= np.arange(LEN)[None, :]).astype(np.float32),
        "c_cos": np.cos(angle).astype(np.float32),
        "c_sin": np.sin(angle).astype(np.float32),
    }


def kernel(**inputs):
    import concourse.bacc as bacc
    from concourse.bass_utils import run_bass_kernel_spmd

    nc = bacc.Bacc("TRN2", target_bir_lowering=False, num_devices=1)
    arrays, aps = {}, {}
    for name, value in {**inputs, **constants()}.items():
        value = np.ascontiguousarray(value)
        arrays[f"in_{name}"] = value
        aps[name] = nc.dram_tensor(f"in_{name}", value.shape, mybir.dt.from_np(value.dtype),
                                   kind="ExternalInput").ap()
    out = nc.dram_tensor("out_0", (SEQS, LEN, DIM), F32, kind="ExternalOutput").ap()
    build(nc, aps, out)
    result = run_bass_kernel_spmd(nc, [arrays], core_ids=[0])
    return result.results[0]["out_0"]
```

```python
from contextlib import ExitStack

import numpy as np

import concourse.bass as bass
from concourse import mybir

F32 = mybir.dt.float32
BF16 = mybir.dt.bfloat16
I32 = mybir.dt.int32
ALU = mybir.AluOpType
ACT = mybir.ActivationFunctionType
AX_X = mybir.AxisListType.X

P = 128
SEQS, LEN, DIM = 128, 64, 128
HEADS, HD = 16, 8
HID = 512
PAIRS = SEQS * LEN // P
STREAMS = 8
ROUNDS = PAIRS // STREAMS
LAYERS = 7
PER_ROUND = LAYERS * STREAMS
QUADS, SLOTS = 4, 4
HALVES = 2
HCH = HID // P
UP, DOWN = 2, 4
SCALE = float(HD) ** -0.5
MASKED = -1e30

L0_SELF, L0_CROSS, L1_CROSS, L2_SELF, L2_CROSS, L3_SELF, L3_CROSS = range(LAYERS)
CROSS = {L0_CROSS, L1_CROSS, L2_CROSS, L3_CROSS}
PRE_NORM = {L0_SELF: 1e-5, L0_CROSS: 1e-5, L1_CROSS: 1e-6, L3_SELF: 1e-6, L3_CROSS: 1e-6}
POST_NORM = {L2_SELF: (0, 1e-5), L2_CROSS: (1, 1e-5)}
MLP = {L0_CROSS: 0, L2_CROSS: 1, L3_CROSS: 2}
MLP_PRE_NORM = {L0_CROSS: 1e-5, L3_CROSS: 1e-6}
MLP_POST_NORM = {L2_CROSS: (2, 1e-6)}
GELU = {L0_CROSS: ACT.Gelu, L2_CROSS: ACT.Gelu, L3_CROSS: ACT.Gelu_apprx_tanh}
Q_BIAS = {L0_SELF, L0_CROSS, L3_SELF, L3_CROSS}
K_BIAS = {L0_SELF, L3_SELF, L3_CROSS}
MASK = {L0_SELF: 0, L2_SELF: 1, L2_CROSS: 2}
ROW_SCALE = {L2_SELF: 0, L2_CROSS: 1}


def layer_of(j):
    return (j % PER_ROUND) // STREAMS


class Norm:

    def __init__(self, sb, name, steps, root):
        self.stats = sb(f"{name}_stats", [P, 6])
        self.mean_var = sb(f"{name}_mean_var", [P, 2])
        self.mean_sq = sb(f"{name}_mean_sq", [P, 1])
        self.var_eps = sb(f"{name}_var_eps", [P, 1])
        self.rstd = sb(f"{name}_rstd", [P, 1])
        self.normed = sb(f"{name}_normed", [P, DIM])
        self.steps, self.root = steps, root


class Signal:

    def __init__(self, sem, per_layer):
        self.sem = sem
        self.per_layer = [per_layer.get(layer, 0) if isinstance(per_layer, dict) else per_layer
                          for layer in range(LAYERS)]
        self.round = STREAMS * sum(self.per_layer)

    def at(self, r, j, m=None):
        full, rest = divmod(j, PER_ROUND)
        before = full * self.round + sum(self.per_layer[layer_of(i)] for i in range(rest))
        return r * self.round + (before + (self.per_layer[layer_of(j)] if m is None else m))


def build(nc, a, out):
    ctx = ExitStack()
    with ctx:
        def sb(name, shape, dt=F32):
            return ctx.enter_context(nc.sbuf_tensor(name, shape, dt))

        def sem(name):
            return ctx.enter_context(nc.semaphore(name))

        def signal(name, per_layer=1):
            return Signal(sem(name), per_layer)

        ident = sb("ident", [P, P])
        ident_bf = sb("ident_bf", [P, P], BF16)
        slot_mask = sb("slot_mask", [P, SLOTS])
        causal = sb("causal", [P, LEN])
        rope_cos = sb("rope_cos", [P, LEN])
        rope_sin = sb("rope_sin", [P, LEN])
        w_q = sb("w_q", [P, LAYERS, DIM])
        w_k = sb("w_k", [P, LAYERS, DIM])
        w_v = sb("w_v", [P, LAYERS, DIM])
        w_o = sb("w_o", [P, LAYERS, DIM])
        w_q_rot = sb("w_q_rot", [P, DIM])
        w_k_rot = sb("w_k_rot", [P, DIM])
        w_1 = sb("w_1", [P, len(MLP), HID])
        w_2 = sb("w_2", [P, len(MLP), HCH, DIM])
        b_q = sb("b_q", [P, LAYERS])
        b_k = sb("b_k", [P, LAYERS])
        b_v = sb("b_v", [P, LAYERS])
        b_1 = sb("b_1", [P, len(MLP), HCH])
        b_o_rows = sb("b_o_rows", [P, LAYERS, DIM])
        b_2_rows = sb("b_2_rows", [P, len(MLP), DIM])
        post_g = sb("post_g", [P, 3, DIM])
        post_b = sb("post_b", [P, 3, DIM])
        mask_int = sb("mask_int", [P, LEN], I32)
        mask_f = sb("mask_f", [P, LEN])
        mask_bias = sb("mask_bias", [P, 3, LEN], BF16)
        row_scale = sb("row_scale", [P, 2])
        raw = sb("raw", [P, 20, DIM])
        raw_t = sb("raw_t", [P, 8, DIM])
        vecs = sb("vecs", [P, 8])
        b_v_wide = sb("b_v_wide", [P, 3, P])
        valid = sb("valid", [P, LEN])

        x_in = sb("x_in", [P, STREAMS, DIM])
        ctx_in = sb("ctx_in", [P, STREAMS, DIM])
        x = sb("x", [P, STREAMS, DIM])
        x_bias = sb("x_bias", [P, STREAMS, DIM])
        ctx_t = sb("ctx_t", [P, STREAMS, 2, 2, LEN])
        q_quads = sb("q_quads", [P, STREAMS, QUADS, P])
        k_slots = sb("k_slots", [P, STREAMS, SLOTS, P])
        v_ones = sb("v_ones", [P, STREAMS, 2, HEADS // 2, 32])
        row_max = sb("row_max", [P, HALVES, 8])
        scaled_max = sb("scaled_max", [P, HALVES, 8])
        shifted = sb("shifted", [P, HALVES, 512])
        probs = sb("probs", [P, HALVES, 4, P])
        pv_sb = sb("pv_sb", [P, HALVES, P])
        recip = sb("recip", [P, HEADS])
        attn = sb("attn", [P, DIM])
        attn_t = sb("attn_t", [P, P])
        minus_half = sb("minus_half", [P, 1])
        h_t = sb("h_t", [P, 2, 2, LEN])
        mlp_h_t = sb("mlp_h_t", [P, P])
        gelu = sb("gelu", [P, 2, HCH, P])
        rope_a = sb("rope_a", [P, 2, P])
        rope_b = sb("rope_b", [P, 2, P])
        rope_qk = sb("rope_qk", [P, 2, P])

        def bank(name):
            return ctx.enter_context(nc.psum_tensor(name, [P, 512], F32))

        ps_scores = [bank("ps_scores0"), bank("ps_scores1")]
        ps_scores_t = bank("ps_scores_t")
        ps_post = bank("ps_post")
        ps_pre = bank("ps_pre")
        ps_q = bank("ps_q")
        ps_k = bank("ps_k")
        ps_hidden = [bank("ps_hidden"), ps_q]

        first_in = sem("first_in")
        first_in_pool = sem("first_in_pool")
        consts_in_pool = sem("consts_in_pool")
        consts_in = sem("consts_in")
        setup_mem = sem("setup_mem")
        setup_pe = sem("setup_pe")
        setup_dve = sem("setup_dve")
        first = {L0_SELF: 1}
        x_loaded = [signal(f"x_loaded{s}") for s in range(STREAMS)]
        ctx_loaded = [signal(f"ctx_loaded{s}") for s in range(STREAMS)]
        stored = [signal(f"stored{s}") for s in range(STREAMS)]
        scores_ready = signal("scores_ready", HALVES)
        scores_t_ready = signal("scores_t_ready", HALVES)
        pv_ready = signal("pv_ready")
        pv_t_ready = signal("pv_t_ready")
        attn_t_ready = signal("attn_t_ready")
        y_ready = signal("y_ready")
        mlp_t_ready = signal("mlp_t_ready", {n: 1 for n in MLP})
        hidden_ready = signal("hidden_ready", {n: 1 for n in MLP})
        mlp_y_ready = signal("mlp_y_ready", {n: 1 for n in MLP})
        h_t_ready = signal("h_t_ready")
        ctx_t_ready = signal("ctx_t_ready", first)
        q_ready = signal("q_ready")
        k_ready = signal("k_ready")
        v_ready = signal("v_ready")
        max_done = signal("max_done", {n: 4 if n in ROW_SCALE else 2 for n in range(LAYERS)})
        shifted_ready = signal("shifted_ready", HALVES)
        recip_done = signal("recip_done")
        attn_ready = signal("attn_ready")
        x_ready = signal("x_ready")
        post_steps = signal("post_steps", {n: 5 for n in POST_NORM})
        mlp_steps = signal("mlp_steps", {n: 2 for n in MLP_PRE_NORM})
        mlp_h_ready = signal("mlp_h_ready", {n: 1 for n in MLP_PRE_NORM})
        mlp_x_ready = signal("mlp_x_ready", {n: 1 for n in MLP})
        mlp_post_steps = signal("mlp_post_steps", {n: 5 for n in MLP_POST_NORM})
        pre_steps = signal("pre_steps", {n: 3 if n == L1_CROSS else 2 for n in PRE_NORM})
        h_ready = signal("h_ready", {n: 1 for n in PRE_NORM})
        rope_steps = signal("rope_steps", {L1_CROSS: 4})
        rope_ready = signal("rope_ready", {L1_CROSS: 1})
        k_slots_ready = signal("k_slots_ready")
        probs_ready = signal("probs_ready", HALVES)
        pv_copied = signal("pv_copied")
        attn_t_copied = signal("attn_t_copied")
        mlp_t_copied = signal("mlp_t_copied", {n: 1 for n in MLP})
        gelu_ready = signal("gelu_ready", {n: 1 for n in MLP})
        h_t_copied = signal("h_t_copied")
        ctx_t_copied = signal("ctx_t_copied", first)
        q_quads_ready = signal("q_quads_ready")
        v_ready_sb = signal("v_ready_sb")
        post_rstd = signal("post_rstd", {n: 1 for n in POST_NORM})
        mlp_rstd = signal("mlp_rstd", {n: 1 for n in MLP_PRE_NORM})
        mlp_post_rstd = signal("mlp_post_rstd", {n: 1 for n in MLP_POST_NORM})
        pre_rstd = signal("pre_rstd", {n: 1 for n in PRE_NORM})
        pre_norm = Norm(sb, "pre", pre_steps, pre_rstd)
        mlp_norm = Norm(sb, "mlp", mlp_steps, mlp_rstd)
        post_norm = Norm(sb, "post", post_steps, post_rstd)
        mlp_post_norm = Norm(sb, "mlp_post", mlp_post_steps, mlp_post_rstd)
        x_bias_ready = signal("x_bias_ready")
        mlp_x_bias_ready = signal("mlp_x_bias_ready", {n: 1 for n in MLP})

        x_dram = a["x"].rearrange("(n two) t c -> n (two t) c", two=2)
        ctx_dram = a["ctx_1024"].rearrange("(n two) t c -> n (two t) c", two=2)
        out_dram = out.rearrange("(n two) t c -> n (two t) c", two=2)

        def rounds(eng, phase):
            for j in range(-1, STREAMS - 1):
                phase(0, j)
            with eng.Fori(0, ROUNDS - 1) as r:
                for j in range(STREAMS - 1, STREAMS - 1 + PER_ROUND):
                    phase(r, j)
            for j in range(STREAMS - 1, PER_ROUND + STREAMS - 1):
                phase(ROUNDS - 1, j)

        def exists(r, j):
            return not isinstance(r, int) or 0 <= PER_ROUND * r + j < PER_ROUND * ROUNDS

        def has_mlp(r, j):
            return exists(r, j) and layer_of(j) in MLP

        def load_count(r, j):
            return r * 16 + (16 * (j // PER_ROUND) + 16)

        def first_round(r, j):
            return isinstance(r, int) and PER_ROUND * r + j < STREAMS

        def residual_read(r, j):
            if layer_of(j) in POST_NORM:
                return post_steps.sem, post_steps.at(r, j, 1)
            return x_ready.sem, x_ready.at(r, j)

        def mlp_residual_read(r, j):
            if layer_of(j) in MLP_POST_NORM:
                return mlp_post_steps.sem, mlp_post_steps.at(r, j, 1)
            return mlp_x_ready.sem, mlp_x_ready.at(r, j)

        def last_x_signal(layer):
            return mlp_x_ready if layer in MLP else x_ready

        def col(name, lo=0):
            return a[name][lo:lo + P].unsqueeze(1)

        def row(name):
            return a[name].unsqueeze(0).to_broadcast([P, DIM])

        def chunks(name, n):
            return a[name].rearrange("(n p) c -> p n c", p=P) if n > 1 else a[name]

        loads = [
            (ident[:, :], a["c_ident"]),
            (raw[:, 0:3, :], chunks("L0_xattn_w_qkv", 3)), (raw[:, 3, :], a["L0_xattn_w_q"]),
            (raw[:, 4:8, :], chunks("L0_xattn_w_fc1", 4)), (raw[:, 8, :], a["L1_xattn_Wq"]),
            (raw[:, 9, :], a["L0_xattn_w_prj1"]), (raw[:, 10, :], a["L0_xattn_w_prj2"]),
            (raw[:, 11:13, :], chunks("L0_xattn_w_kv", 2)), (raw[:, 13:15, :], chunks("L1_xattn_Wkv", 2)),
            (raw[:, 15, :], a["L1_xattn_Wo"]),
            (raw[:, 16:20, :], a["L0_xattn_w_fc2"].rearrange("p (n c) -> p n c", c=P)),
            (vecs[:, 0:1], col("L0_xattn_ln1_g")), (vecs[:, 1:2], col("L0_xattn_ln1_b")),
            (vecs[:, 2:3], col("L0_xattn_ln2_g")), (vecs[:, 3:4], col("L0_xattn_ln2_b")),
            (vecs[:, 4:5], col("L0_xattn_ln3_g")), (vecs[:, 5:6], col("L0_xattn_ln3_b")),
            (vecs[:, 6:7], col("L1_xattn_norm_w")),
        ]
        N_FIRST = len(loads)
        loads += [
            (slot_mask[:, :], a["c_slot"]), (causal[:, :], a["c_causal"]),
            (rope_cos[:, :], a["c_cos"]), (rope_sin[:, :], a["c_sin"]),
            (w_q[:, 3, :], a["L2_xattn_Wqkv"][:, 0:128]), (w_k[:, 3, :], a["L2_xattn_Wqkv"][:, 128:256]),
            (w_v[:, 3, :], a["L2_xattn_Wqkv"][:, 256:384]), (w_o[:, 3, :], a["L2_xattn_Wo1"]),
            (w_q[:, 4, :], a["L2_xattn_Wq"]), (w_k[:, 4, :], a["L2_xattn_Wk"]),
            (w_v[:, 4, :], a["L2_xattn_Wv"]), (w_o[:, 4, :], a["L2_xattn_Wo2"]),
            (w_q[:, 5, :], a["L3_xattn_Wqkv"][:, 0:128]), (w_k[:, 5, :], a["L3_xattn_Wqkv"][:, 128:256]),
            (w_v[:, 5, :], a["L3_xattn_Wqkv"][:, 256:384]), (w_o[:, 5, :], a["L3_xattn_Wos"]),
            (w_q[:, 6, :], a["L3_xattn_Wq"]), (w_k[:, 6, :], a["L3_xattn_Wkv"][:, 0:128]),
            (w_v[:, 6, :], a["L3_xattn_Wkv"][:, 128:256]), (w_o[:, 6, :], a["L3_xattn_Woc"]),
            (w_1[:, 1, :], a["L2_xattn_W1"]), (w_1[:, 2, :], a["L3_xattn_W1"]),
            (w_2[:, 1, :, :], chunks("L2_xattn_W2", 4)), (w_2[:, 2, :, :], chunks("L3_xattn_W2", 4)),
            (b_q[:, 5:6], col("L3_xattn_bqkv")), (b_k[:, 5:6], col("L3_xattn_bqkv", 128)),
            (b_v[:, 5:6], col("L3_xattn_bqkv", 256)), (b_q[:, 6:7], col("L3_xattn_bq")),
            (b_k[:, 6:7], col("L3_xattn_bkv")), (b_v[:, 6:7], col("L3_xattn_bkv", 128)),
            (b_o_rows[:, 0, :], row("L0_xattn_b_prj1")), (b_o_rows[:, 1, :], row("L0_xattn_b_prj2")),
            (b_o_rows[:, 3, :], row("L2_xattn_bo1")), (b_o_rows[:, 4, :], row("L2_xattn_bo2")),
            (b_o_rows[:, 5, :], row("L3_xattn_bos")), (b_o_rows[:, 6, :], row("L3_xattn_boc")),
            (b_2_rows[:, 0, :], row("L0_xattn_b_fc2")), (b_2_rows[:, 1, :], row("L2_xattn_bf2")),
            (b_2_rows[:, 2, :], row("L3_xattn_b2")),
            (post_g[:, 0, :], row("L2_xattn_g1")), (post_g[:, 1, :], row("L2_xattn_g2")),
            (post_g[:, 2, :], row("L2_xattn_g3")), (post_b[:, 0, :], row("L2_xattn_b1")),
            (post_b[:, 1, :], row("L2_xattn_b2")), (post_b[:, 2, :], row("L2_xattn_b3")),
            (mask_int[:, :], a["mask_1xS2_if1"].to_broadcast([P, LEN])),
        ]
        for m, name in enumerate(("L0_xattn_b_fc1", "L2_xattn_bf1", "L3_xattn_b1")):
            for c in range(HCH):
                loads.append((b_1[:, m, c:c + 1], col(name, c * P)))
        N_LOADS = len(loads)

        def load_constants(eng, which):
            for n in range(which, N_LOADS, 3):
                done = (first_in_pool if n < N_FIRST else consts_in_pool) if which == 2 else \
                       (first_in if n < N_FIRST else consts_in)
                eng.dma_start(*loads[n]).then_inc(done, 16)

        pool_first, pool_all = len(range(2, N_FIRST, 3)), len(range(2, N_LOADS, 3))

        def wait_first_loads(eng):
            eng.wait_ge(first_in, 16 * (N_FIRST - pool_first))
            eng.wait_ge(first_in_pool, 16 * pool_first)

        def wait_other_loads(eng):
            eng.wait_ge(consts_in, 16 * (N_LOADS - N_FIRST - (pool_all - pool_first)))
            eng.wait_ge(consts_in_pool, 16 * (pool_all - pool_first))

        scaled_to = [(w_q[:, 0, :], 0), (w_k[:, 0, :], 0), (w_v[:, 0, :], 0), (w_q[:, 1, :], 2)] + \
                    [(w_1[:, 0, c * P:(c + 1) * P], 4) for c in range(HCH)] + [(w_q[:, 2, :], 6)]
        copied_to = [w_o[:, 0, :], w_o[:, 1, :], w_k[:, 1, :], w_v[:, 1, :], w_k[:, 2, :], w_v[:, 2, :],
                     w_o[:, 2, :]] + [w_2[:, 0, c, :] for c in range(HCH)]
        setup_banks = [ps_scores[0], ps_scores[1], ps_scores_t, ps_post, ps_pre]

        def setup_psum(n):
            return setup_banks[n // 4][:, (n % 4) * P:(n % 4 + 1) * P]

        N_MEM = 8
        STORED_0 = 1

        with nc.Block() as block:

            @block.sync
            def _(sp):
                load_constants(sp, 0)

                def load(n, s):
                    sp.dma_start(x_in[:, s, :], x_dram[bass.ds(n, 1), :, :].rearrange("n p c -> (n p) c")
                                 if not isinstance(n, int) else x_dram[n]).then_inc(x_loaded[s].sem, 16)
                    sp.dma_start(ctx_in[:, s, :], ctx_dram[bass.ds(n, 1), :, :].rearrange("n p c -> (n p) c")
                                 if not isinstance(n, int) else ctx_dram[n]).then_inc(ctx_loaded[s].sem, 16)

                def store(r, n, s):
                    sp.wait_ge(mlp_x_ready.sem, mlp_x_ready.at(r, PER_ROUND - STREAMS + s))
                    sp.dma_start(out_dram[bass.ds(n, 1), :, :].rearrange("n p c -> (n p) c")
                                 if not isinstance(n, int) else out_dram[n], x[:, s, :]).then_inc(stored[s].sem, 16)

                for s in range(STREAMS):
                    load(s, s)
                with sp.Fori(0, ROUNDS - 1) as r:
                    pair = [sp.snap(STREAMS * r + k) for k in range(2 * STREAMS)]
                    sp.wait_ge(h_ready.sem, h_ready.at(r, STREAMS - 1))
                    sp.wait_ge(x_bias_ready.sem, x_bias_ready.at(r, STREAMS - 1))
                    sp.wait_ge(ctx_t_ready.sem, ctx_t_ready.at(r, STREAMS - 1))
                    for s in range(STREAMS):
                        load(pair[STREAMS + s], s)
                    for s in range(STREAMS):
                        store(r, pair[s], s)
                for s in range(STREAMS):
                    store(ROUNDS - 1, PAIRS - STREAMS + s, s)
                for s in range(STREAMS):
                    sp.wait_ge(stored[s].sem, 16 * ROUNDS + STORED_0)

            @block.gpsimd
            def _(pool):
                load_constants(pool, 2)
                pool.memset(v_ones[:, :, :, :, 0:16], 0.0).then_inc(setup_mem, 1)
                pool.memset(b_o_rows[:, L1_CROSS, :], 0.0).then_inc(setup_mem, 1)
                pool.memset(minus_half[:, :], -0.5).then_inc(setup_mem, 1)
                wait_other_loads(pool)
                pool.wait_ge(setup_dve, SETUP_DVE)

                def inverse_root(r, j, norm, m=None):
                    pool.wait_ge(norm.steps.sem, norm.steps.at(r, j, m))
                    pool.tensor_tensor(norm.rstd[:, :], norm.var_eps[:, :], minus_half[:, :],
                                       ALU.pow).then_inc(norm.root.sem, 1)

                def attention_bias(r, j):
                    layer, s = layer_of(j), j % STREAMS
                    if layer == L0_SELF:
                        pool.wait_ge(x_loaded[s].sem, load_count(r, j))
                        src = x_in
                        if not first_round(r, j):
                            pool.wait_ge(mlp_x_ready.sem, mlp_x_ready.at(r, j - STREAMS))
                    else:
                        done = last_x_signal(layer_of(j - STREAMS))
                        pool.wait_ge(done.sem, done.at(r, j - STREAMS))
                        src = x
                    pool.tensor_tensor(x_bias[:, s, :], src[:, s, :], b_o_rows[:, layer, :],
                                       ALU.add).then_inc(x_bias_ready.sem, 1)

                def mlp_bias(r, j):
                    layer, s = layer_of(j), j % STREAMS
                    pool.wait_ge(x_ready.sem, x_ready.at(r, j))
                    pool.tensor_tensor(x_bias[:, s, :], x[:, s, :], b_2_rows[:, MLP[layer], :],
                                       ALU.add).then_inc(mlp_x_bias_ready.sem, 1)

                def phase(r, j):
                    core, post, pre = exists(r, j), exists(r, j - 1), exists(r, j + 1)
                    up, down, odd = has_mlp(r, j - UP), has_mlp(r, j - DOWN), (j - UP) % 2 == 1
                    if pre and layer_of(j + 1) in PRE_NORM:
                        inverse_root(r, j + 1, pre_norm)
                    if up and layer_of(j - UP) in MLP_PRE_NORM:
                        inverse_root(r, j - UP, mlp_norm)
                    if up:
                        mlp_bias(r, j - UP)
                    if down and layer_of(j - DOWN) in MLP_POST_NORM:
                        inverse_root(r, j - DOWN, mlp_post_norm, 3)
                    if post and layer_of(j - 1) in POST_NORM:
                        inverse_root(r, j - 1, post_norm, 3)
                    if pre:
                        attention_bias(r, j + 1)

                rounds(pool, phase)

            @block.scalar
            def _(act):
                load_constants(act, 1)
                wait_other_loads(act)
                act.wait_ge(setup_mem, N_MEM)
                act.wait_ge(setup_dve, SETUP_DVE)

                def copy_h_t(r, j):
                    act.wait_ge(h_t_ready.sem, h_t_ready.at(r, j))
                    nc.scalar.copy(h_t[:, :, :, :], ps_pre[:, P:2 * P].rearrange("p (b t) -> p b t", b=2)
                                   .unsqueeze(2).to_broadcast([P, 2, 2, LEN])).then_inc(h_t_copied.sem, 1)
                    if layer_of(j) == L0_SELF:
                        act.wait_ge(ctx_t_ready.sem, ctx_t_ready.at(r, j))
                        nc.scalar.copy(ctx_t[:, j % STREAMS, :, :, :], ps_pre[:, 0:P]
                                       .rearrange("p (b t) -> p b t", b=2).unsqueeze(2)
                                       .to_broadcast([P, 2, 2, LEN])).then_inc(ctx_t_copied.sem, 1)

                def copy_q(r, j):
                    layer, s = layer_of(j), j % STREAMS
                    if layer == L1_CROSS:
                        act.wait_ge(rope_ready.sem, rope_ready.at(r, j))
                        src = rope_qk[:, 0, :]
                    else:
                        act.wait_ge(q_ready.sem, q_ready.at(r, j))
                        src = ps_q[:, 0:P]
                    for g in range(QUADS):
                        rows = slice(32 * g, 32 * g + 32)
                        if layer in Q_BIAS:
                            ins = nc.scalar.activation(q_quads[rows, s, g, :], src[rows, :], ACT.Identity,
                                                       bias=b_q[rows, layer:layer + 1])
                        else:
                            ins = nc.scalar.copy(q_quads[rows, s, g, :], src[rows, :])
                    ins.then_inc(q_quads_ready.sem, 1)

                def copy_v(r, j):
                    s = j % STREAMS
                    act.wait_ge(v_ready.sem, v_ready.at(r, j))
                    for e in range(2):
                        rows = slice(64 * e, 64 * e + 64)
                        ins = nc.scalar.copy(
                            v_ones[rows, s, :, :, HD * e:HD * e + HD].rearrange("p b h d -> p (b h) d"),
                            ps_pre[rows, 256:512].rearrange("p (bh e d) -> p bh e d", e=2, d=HD)[:, :, e, :])
                    ins.then_inc(v_ready_sb.sem, 1)

                def copy_pv(r, j):
                    act.wait_ge(pv_ready.sem, pv_ready.at(r, j))
                    nc.scalar.copy(pv_sb[:, :, :], ps_post[:, 0:256].rearrange("p (u t) -> p u t", u=2)) \
                        .then_inc(pv_copied.sem, 1)

                def copy_attn_t(r, j):
                    act.wait_ge(attn_t_ready.sem, attn_t_ready.at(r, j))
                    nc.scalar.copy(attn_t[:, :], ps_post[:, 0:P]).then_inc(attn_t_copied.sem, 1)

                def copy_mlp_t(r, j):
                    act.wait_ge(mlp_t_ready.sem, mlp_t_ready.at(r, j))
                    nc.scalar.copy(mlp_h_t[:, :], ps_pre[:, 0:P]).then_inc(mlp_t_copied.sem, 1)

                def gelus(r, j):
                    layer = layer_of(j)
                    act.wait_ge(hidden_ready.sem, hidden_ready.at(r, j))
                    for c in range(HCH):
                        ins = nc.scalar.activation(gelu[:, j % 2, c, :], ps_hidden[j % 2][:, c * P:(c + 1) * P], GELU[layer],
                                                   bias=b_1[:, MLP[layer], c:c + 1])
                    ins.then_inc(gelu_ready.sem, 1)

                def exps(r, j, u):
                    act.wait_ge(scores_t_ready.sem, scores_t_ready.at(r, j, u + 1))
                    nc.scalar.activation(probs[:, u, :, :], ps_scores_t[:, :]
                                         .rearrange("p (h t) -> p h t", h=4), ACT.Exp,
                                         scale=SCALE).then_inc(probs_ready.sem, 1)

                def phase(r, j):
                    core, post, pre = exists(r, j), exists(r, j - 1), exists(r, j + 1)
                    up, down, odd = has_mlp(r, j - UP), has_mlp(r, j - DOWN), (j - UP) % 2 == 1
                    if post:
                        copy_pv(r, j - 1)
                    if (j - 1 - UP) % 2 == 1 and has_mlp(r, j - 1 - UP):
                        gelus(r, j - 1 - UP)
                    if up:
                        copy_mlp_t(r, j - UP)
                    if pre:
                        copy_h_t(r, j + 1)
                    if core:
                        exps(r, j, 0)
                    if post:
                        copy_attn_t(r, j - 1)
                    if pre:
                        copy_q(r, j + 1)
                        copy_v(r, j + 1)
                    if core:
                        exps(r, j, 1)
                    if up and odd:
                        gelus(r, j - UP - 1)

                rounds(act, phase)

            @block.tensor
            def _(pe):
                wait_first_loads(pe)
                for n in range(20):
                    ins = nc.tensor.transpose(setup_psum(n), raw[:, n, :], ident[:, :])
                ins.then_inc(setup_pe, 1)
                pe.wait_ge(setup_dve, SETUP_RAW_T)
                for i, (n, vec) in enumerate(((0, 1), (1, 1), (2, 1), (3, 3), (4, 5), (5, 5), (6, 5), (7, 5))):
                    ins = nc.tensor.matmul(ps_q[:, i:i + 1], raw_t[:, n, :], vecs[:, vec:vec + 1],
                                           start=True, stop=True)
                ins.then_inc(setup_pe, 1)
                pe.wait_ge(setup_dve, SETUP_WIDE)
                for i, layer in enumerate((0, 5, 6)):
                    ins = nc.tensor.matmul(ps_k[:, i * P:(i + 1) * P], b_v_wide[:, i, :], w_o[:, layer, :],
                                           start=True, stop=True)
                ins.then_inc(setup_pe, 1)
                pe.wait_ge(setup_dve, SETUP_DVE)
                pe.wait_ge(setup_mem, N_MEM)

                def bank_pre_free(r, j):
                    if exists(r, j - 1):
                        pe.wait_ge(v_ready_sb.sem, v_ready_sb.at(r, j - 1))
                    if has_mlp(r, j - 1 - UP):
                        pe.wait_ge(mlp_t_copied.sem, mlp_t_copied.at(r, j - 1 - UP))

                def pre_h(r, j):
                    layer, s = layer_of(j), j % STREAMS
                    if layer in PRE_NORM:
                        pe.wait_ge(h_ready.sem, h_ready.at(r, j))
                        src = pre_norm.normed[:, :]
                    else:
                        done = last_x_signal(layer_of(j - STREAMS))
                        pe.wait_ge(done.sem, done.at(r, j - STREAMS))
                        src = x[:, s, :]
                    bank_pre_free(r, j)
                    nc.tensor.transpose(ps_pre[:, P:2 * P], src, ident[:, :]).then_inc(h_t_ready.sem, 1)
                    if layer == L0_SELF:
                        pe.wait_ge(ctx_loaded[s].sem, load_count(r, j))
                        pe.wait_ge(h_t_copied.sem, h_t_copied.at(r, j))
                        nc.tensor.transpose(ps_pre[:, 0:P], ctx_in[:, s, :], ident[:, :]) \
                            .then_inc(ctx_t_ready.sem, 1)

                def pre_qk(r, j):
                    layer, s = layer_of(j), j % STREAMS
                    pe.wait_ge(h_t_copied.sem, h_t_copied.at(r, j))
                    tokens = h_t[:, :, 0, :]
                    kv_tokens = ctx_t[:, s, :, 0, :] if layer in CROSS else tokens
                    if (j - UP - 2) % 2 == 1 and has_mlp(r, j - UP - 2):
                        pe.wait_ge(gelu_ready.sem, gelu_ready.at(r, j - UP - 2))
                    ins = nc.tensor.matmul(ps_q[:, 0:P], w_q[:, layer, :], tokens, start=True, stop=True)
                    if layer == L1_CROSS:
                        ins = nc.tensor.matmul(ps_q[:, P:2 * P], w_q_rot[:, :], tokens, start=True, stop=True)
                    ins.then_inc(q_ready.sem, 1)
                    if has_mlp(r, j - DOWN - 1):
                        pe.wait_ge(*mlp_residual_read(r, j - DOWN - 1))
                    ins = nc.tensor.matmul(ps_k[:, 0:P], w_k[:, layer, :], kv_tokens, start=True, stop=True)
                    if layer == L1_CROSS:
                        ins = nc.tensor.matmul(ps_k[:, P:2 * P], w_k_rot[:, :], kv_tokens, start=True, stop=True)
                    ins.then_inc(k_ready.sem, 1)

                def pre_v(r, j):
                    layer, s = layer_of(j), j % STREAMS
                    if layer == L0_SELF:
                        pe.wait_ge(ctx_t_copied.sem, ctx_t_copied.at(r, j))
                    for b in range(2):
                        src = ctx_t[:, s, b, :, :] if layer in CROSS else h_t[:, b, :, :]
                        ins = nc.tensor.matmul(ps_pre[:, 256 + b * P:256 + (b + 1) * P],
                                               src.rearrange("p k t -> p (k t)"), w_v[:, layer, :],
                                               start=True, stop=True)
                    ins.then_inc(v_ready.sem, 1)

                def scores(r, j, u):
                    layer, s = layer_of(j), j % STREAMS
                    if u == 0:
                        pe.wait_ge(q_quads_ready.sem, q_quads_ready.at(r, j))
                        pe.wait_ge(k_slots_ready.sem, k_slots_ready.at(r, j))
                    for g in (2 * u, 2 * u + 1):
                        cols = slice((g % 2) * 256, (g % 2) * 256 + 256)
                        for b in range(2):
                            ins = nc.tensor.matmul(ps_scores[u][64 * b:64 * b + 64, cols],
                                                   q_quads[:, s, g, 64 * b:64 * b + 64],
                                                   k_slots[:, s, :, 64 * b:64 * b + 64],
                                                   start=True, stop=layer not in MASK)
                        if layer in MASK:
                            for b in range(2):
                                ins = nc.tensor.matmul(ps_scores[u][64 * b:64 * b + 64, cols],
                                                       ident_bf[:, 64 * b:64 * b + 64],
                                                       mask_bias[:, MASK[layer], :].unsqueeze(1)
                                                       .to_broadcast([P, SLOTS, LEN]),
                                                       start=False, stop=True)
                    ins.then_inc(scores_ready.sem, 1)

                def transposes(r, j, u):
                    pe.wait_ge(shifted_ready.sem, shifted_ready.at(r, j, u + 1))
                    if u:
                        pe.wait_ge(probs_ready.sem, probs_ready.at(r, j, u))
                    for h in range(4):
                        ins = nc.tensor.transpose(ps_scores_t[:, h * P:(h + 1) * P],
                                                  shifted[:, u, h * P:(h + 1) * P], ident[:, :])
                    ins.then_inc(scores_t_ready.sem, 1)

                def values(r, j, u):
                    s = j % STREAMS
                    if u == 0:
                        pe.wait_ge(v_ready_sb.sem, v_ready_sb.at(r, j))
                        if exists(r, j - 1):
                            pe.wait_ge(*residual_read(r, j - 1))
                    pe.wait_ge(probs_ready.sem, probs_ready.at(r, j, u + 1))
                    for b in range(2):
                        for h in range(4):
                            ins = nc.tensor.matmul(ps_post[32 * h:32 * h + 32, u * P + 64 * b:u * P + 64 * b + 64],
                                                   v_ones[:, s, b, 4 * u + h, :],
                                                   probs[:, u, h, 64 * b:64 * b + 64], start=True, stop=True)
                    if u == HALVES - 1:
                        ins.then_inc(pv_ready.sem, 1)

                def pv_t(r, j):
                    pe.wait_ge(pv_copied.sem, pv_copied.at(r, j))
                    for u in range(HALVES):
                        ins = nc.tensor.transpose(ps_post[:, 256 + u * P:256 + (u + 1) * P], pv_sb[:, u, :],
                                                  ident[:, :])
                    ins.then_inc(pv_t_ready.sem, 1)

                def attn_turn(r, j):
                    pe.wait_ge(attn_ready.sem, attn_ready.at(r, j))
                    nc.tensor.transpose(ps_post[:, 0:P], attn[:, :], ident[:, :]) \
                        .then_inc(attn_t_ready.sem, 1)

                def project(r, j):
                    pe.wait_ge(attn_t_copied.sem, attn_t_copied.at(r, j))
                    nc.tensor.matmul(ps_post[:, P:2 * P], attn_t[:, :], w_o[:, layer_of(j), :],
                                     start=True, stop=True).then_inc(y_ready.sem, 1)

                def mlp_turn(r, j):
                    layer, s = layer_of(j), j % STREAMS
                    if layer in MLP_PRE_NORM:
                        pe.wait_ge(mlp_h_ready.sem, mlp_h_ready.at(r, j))
                        src = mlp_norm.normed[:, :]
                    else:
                        pe.wait_ge(x_ready.sem, x_ready.at(r, j))
                        src = x[:, s, :]
                    if exists(r, j + UP):
                        pe.wait_ge(v_ready_sb.sem, v_ready_sb.at(r, j + UP))
                    nc.tensor.transpose(ps_pre[:, 0:P], src, ident[:, :]).then_inc(mlp_t_ready.sem, 1)

                def mlp_up(r, j):
                    pe.wait_ge(mlp_t_copied.sem, mlp_t_copied.at(r, j))
                    if j % 2 == 1 and exists(r, j + UP + 1):
                        pe.wait_ge(q_quads_ready.sem, q_quads_ready.at(r, j + UP + 1))
                    for c in range(HCH):
                        ins = nc.tensor.matmul(ps_hidden[j % 2][:, c * P:(c + 1) * P],
                                               w_1[:, MLP[layer_of(j)], c * P:(c + 1) * P], mlp_h_t[:, :],
                                               start=True, stop=True)
                    ins.then_inc(hidden_ready.sem, 1)

                def mlp_down(r, j):
                    pe.wait_ge(gelu_ready.sem, gelu_ready.at(r, j))
                    if exists(r, j + DOWN):
                        pe.wait_ge(k_slots_ready.sem, k_slots_ready.at(r, j + DOWN))
                    else:
                        pe.wait_ge(*mlp_residual_read(r, j - 1))
                    for c in range(HCH):
                        ins = nc.tensor.matmul(ps_k[:, 256:384], gelu[:, j % 2, c, :], w_2[:, MLP[layer_of(j)], c, :],
                                               start=c == 0, stop=c == HCH - 1)
                    ins.then_inc(mlp_y_ready.sem, 1)

                def phase(r, j):
                    core, post, pre = exists(r, j), exists(r, j - 1), exists(r, j + 1)
                    up, down, odd = has_mlp(r, j - UP), has_mlp(r, j - DOWN), (j - UP) % 2 == 1
                    if core:
                        scores(r, j, 0)
                    if post:
                        values(r, j - 1, 0)
                        values(r, j - 1, 1)
                    if core:
                        scores(r, j, 1)
                    if up:
                        mlp_turn(r, j - UP)
                    if post:
                        pv_t(r, j - 1)
                    if pre:
                        pre_h(r, j + 1)
                    if core:
                        transposes(r, j, 0)
                    if down:
                        mlp_down(r, j - DOWN)
                    if post:
                        attn_turn(r, j - 1)
                    if up and not odd:
                        mlp_up(r, j - UP)
                    if pre:
                        pre_qk(r, j + 1)
                    if post:
                        project(r, j - 1)
                    if pre:
                        pre_v(r, j + 1)
                    if core:
                        transposes(r, j, 1)
                    if up and odd:
                        mlp_up(r, j - UP)

                rounds(pe, phase)

            @block.vector
            def _(dve):
                v = nc.vector
                v.memset(q_quads[:, :, :, :], 0.0).then_inc(setup_mem, 1)
                for rows, one, zero in ((slice(0, 64), 16, 24), (slice(64, 128), 24, 16)):
                    v.memset(v_ones[rows, :, :, :, one:one + HD], 1.0).then_inc(setup_mem, 1)
                    v.memset(v_ones[rows, :, :, :, zero:zero + HD], 0.0).then_inc(setup_mem, 1)
                wait_first_loads(dve)
                for s in range(STREAMS):
                    v.memset(x[:, s, 0:1], 0.0).then_inc(stored[s].sem, STORED_0)
                done = [0]

                def step(ins):
                    done[0] += 1
                    ins.then_inc(setup_dve, 1)

                def settle():
                    dve.wait_ge(setup_dve, done[0])

                dve.wait_ge(setup_pe, 1)
                for n in range(8):
                    step(v.tensor_copy(raw_t[:, n, :], setup_psum(n)))
                assert done[0] == SETUP_RAW_T
                for n, (dst, vec) in enumerate(scaled_to):
                    step(v.tensor_scalar(dst, setup_psum(n), vecs[:, vec:vec + 1], None, ALU.mult))
                for n, dst in enumerate(copied_to):
                    step(v.tensor_copy(dst, setup_psum(len(scaled_to) + n)))
                dve.wait_ge(setup_pe, 2)
                wait_other_loads(dve)
                dve.wait_ge(setup_mem, N_MEM)
                step(v.tensor_copy(b_q[:, 0:1], ps_q[:, 0:1]))
                step(v.tensor_copy(b_k[:, 0:1], ps_q[:, 1:2]))
                step(v.tensor_copy(b_v[:, 0:1], ps_q[:, 2:3]))
                step(v.tensor_copy(b_q[:, 1:2], ps_q[:, 3:4]))
                step(v.tensor_tensor(b_1[:, 0, :], ps_q[:, 4:8], b_1[:, 0, :], ALU.add))
                settle()
                for i, layer in enumerate((0, 5, 6)):
                    step(v.tensor_copy(b_v_wide[:, i, :], b_v[:, layer:layer + 1].to_broadcast([P, P])))
                assert done[0] == SETUP_WIDE
                for w, w_rot in ((w_q, w_q_rot), (w_k, w_k_rot)):
                    src = w[:, L1_CROSS, :].rearrange("p (h a d) -> p h a d", a=2, d=HD // 2)
                    dst = w_rot[:, :].rearrange("p (h a d) -> p h a d", a=2, d=HD // 2)
                    step(v.tensor_scalar(dst[:, :, 0, :], src[:, :, 1, :], -1.0, None, ALU.mult))
                    step(v.tensor_copy(dst[:, :, 1, :], src[:, :, 0, :]))
                step(v.tensor_copy(ident_bf[:, :], ident[:, :]))
                step(v.tensor_copy(mask_f[:, :], mask_int[:, :]))
                step(v.tensor_scalar(mask_bias[:, 0, :], causal[:, :], -1.0, -MASKED, ALU.add, ALU.mult))
                settle()
                step(v.tensor_tensor(valid[:, :], causal[:, :], mask_f[:, :], ALU.mult))
                settle()
                for i, src in enumerate((valid, mask_f)):
                    step(v.tensor_reduce(row_scale[:, i:i + 1], src[:, :], AX_X, ALU.max))
                settle()
                for i, src in enumerate((valid, mask_f)):
                    step(v.tensor_scalar(src[:, :], src[:, :], -1.0, -MASKED, ALU.add, ALU.mult))
                settle()
                for i, src in enumerate((valid, mask_f)):
                    step(v.tensor_scalar(mask_bias[:, 1 + i, :], src[:, :], row_scale[:, i:i + 1], None,
                                         ALU.mult))
                dve.wait_ge(setup_pe, 3)
                for i, layer in enumerate((0, 5, 6)):
                    step(v.tensor_tensor(b_o_rows[:, layer, :], ps_k[:, i * P:(i + 1) * P],
                                         b_o_rows[:, layer, :], ALU.add))
                assert done[0] == SETUP_DVE, done[0]
                settle()

                def norm_begin(r, j, norm, src, eps, at=0, rms=False):
                    v.bn_stats(norm.stats[:, :], src)
                    dve.drain()
                    v.bn_aggr(norm.mean_var[:, :], norm.stats[:, :]).then_inc(norm.steps.sem, 1)
                    dve.wait_ge(norm.steps.sem, norm.steps.at(r, j, at + 1))
                    var = norm.mean_var[:, 1:2]
                    if rms:
                        v.scalar_tensor_tensor(out=norm.mean_sq[:, :], in0=norm.mean_var[:, 0:1],
                                               scalar=norm.mean_var[:, 0:1], in1=var,
                                               op0=ALU.mult, op1=ALU.add).then_inc(norm.steps.sem, 1)
                        dve.wait_ge(norm.steps.sem, norm.steps.at(r, j, at + 2))
                        var = norm.mean_sq[:, :]
                    v.tensor_scalar(norm.var_eps[:, :], var, eps, None, ALU.add).then_inc(norm.steps.sem, 1)

                def norm_end(r, j, norm, src, ready, rms=False):
                    dve.wait_ge(norm.root.sem, norm.root.at(r, j))
                    if rms:
                        ins = v.tensor_scalar(norm.normed[:, :], src, norm.rstd[:, 0:1], None, ALU.mult)
                    else:
                        ins = v.tensor_scalar(norm.normed[:, :], src, norm.mean_var[:, 0:1],
                                              norm.rstd[:, 0:1], ALU.subtract, ALU.mult)
                    ins.then_inc(ready.sem, 1)

                def post_norm_begin(r, j, norm, which):
                    dve.wait_ge(norm.steps.sem, norm.steps.at(r, j, 1))
                    norm_begin(r, j, norm, x[:, j % STREAMS, :], which[1], at=1)

                def post_norm_end(r, j, norm, which, ready):
                    s, g = j % STREAMS, which[0]
                    norm_end(r, j, norm, x[:, s, :], norm.steps)
                    dve.wait_ge(norm.steps.sem, norm.steps.at(r, j, 4))
                    v.tensor_tensor(norm.normed[:, :], norm.normed[:, :], post_g[:, g, :],
                                    ALU.mult).then_inc(norm.steps.sem, 1)
                    dve.wait_ge(norm.steps.sem, norm.steps.at(r, j, 5))
                    v.tensor_tensor(x[:, s, :], norm.normed[:, :], post_b[:, g, :], ALU.add).then_inc(ready.sem, 1)

                def pre_source(j):
                    return (x_in if layer_of(j) == L0_SELF else x)[:, j % STREAMS, :]

                def pre_norm_begin(r, j):
                    layer, s = layer_of(j), j % STREAMS
                    if layer not in PRE_NORM:
                        return
                    if layer == L0_SELF:
                        dve.wait_ge(x_loaded[s].sem, load_count(r, j))
                    else:
                        before = last_x_signal(layer_of(j - STREAMS))
                        dve.wait_ge(before.sem, before.at(r, j - STREAMS))
                    norm_begin(r, j, pre_norm, pre_source(j), PRE_NORM[layer], rms=layer == L1_CROSS)

                def pre_norm_end(r, j):
                    layer = layer_of(j)
                    if layer in PRE_NORM:
                        norm_end(r, j, pre_norm, pre_source(j), h_ready, rms=layer == L1_CROSS)

                def mlp_norm_begin(r, j):
                    if layer_of(j) in MLP_PRE_NORM:
                        dve.wait_ge(x_ready.sem, x_ready.at(r, j))
                        norm_begin(r, j, mlp_norm, x[:, j % STREAMS, :], MLP_PRE_NORM[layer_of(j)])

                def mlp_norm_end(r, j):
                    if layer_of(j) in MLP_PRE_NORM:
                        norm_end(r, j, mlp_norm, x[:, j % STREAMS, :], mlp_h_ready)

                def pre_k(r, j):
                    layer, s = layer_of(j), j % STREAMS
                    mask = slot_mask[:, :].unsqueeze(2).to_broadcast([P, SLOTS, P])
                    dve.wait_ge(k_ready.sem, k_ready.at(r, j))
                    src = ps_k[:, 0:P]
                    if layer == L1_CROSS:
                        dve.wait_ge(q_ready.sem, q_ready.at(r, j))
                        cos = rope_cos[:, :].unsqueeze(1).to_broadcast([P, 2, LEN])
                        sin = rope_sin[:, :].unsqueeze(1).to_broadcast([P, 2, LEN])

                        def two(t):
                            return t.rearrange("p (b t) -> p b t", b=2)

                        for i, ps in enumerate((ps_q, ps_k)):
                            v.tensor_tensor(two(rope_a[:, i, :]), two(ps[:, 0:P]), cos,
                                            ALU.mult).then_inc(rope_steps.sem, 1)
                            v.tensor_tensor(two(rope_b[:, i, :]), two(ps[:, P:2 * P]), sin,
                                            ALU.mult).then_inc(rope_steps.sem, 1)
                        dve.wait_ge(rope_steps.sem, rope_steps.at(r, j))
                        v.tensor_tensor(rope_qk[:, :, :], rope_a[:, :, :], rope_b[:, :, :],
                                        ALU.add).then_inc(rope_ready.sem, 1)
                        dve.wait_ge(rope_ready.sem, rope_ready.at(r, j))
                        src = rope_qk[:, 1, :]
                    src = src.unsqueeze(1).to_broadcast([P, SLOTS, P])
                    if layer in K_BIAS:
                        ins = v.scalar_tensor_tensor(out=k_slots[:, s, :, :], in0=src,
                                                     scalar=b_k[:, layer:layer + 1], in1=mask,
                                                     op0=ALU.add, op1=ALU.mult)
                    else:
                        ins = v.tensor_tensor(k_slots[:, s, :, :], src, mask, ALU.mult)
                    ins.then_inc(k_slots_ready.sem, 1)

                def shift(r, j, u):
                    layer = layer_of(j)
                    per_half = 2 if layer in ROW_SCALE else 1
                    heads = ps_scores[u][:, :].rearrange("p (h k) -> p h k", k=LEN)
                    dst = shifted[:, u, :].rearrange("p (h k) -> p h k", k=LEN)
                    dve.wait_ge(scores_ready.sem, scores_ready.at(r, j, u + 1))
                    v.tensor_reduce(row_max[:, u, :], heads, AX_X, ALU.max).then_inc(max_done.sem, 1)
                    dve.wait_ge(max_done.sem, max_done.at(r, j, per_half * u + 1))
                    if layer in ROW_SCALE:
                        scale = row_scale[:, ROW_SCALE[layer]:ROW_SCALE[layer] + 1]
                        v.tensor_scalar(scaled_max[:, u, :], row_max[:, u, :], scale, None,
                                        ALU.mult).then_inc(max_done.sem, 1)
                        dve.wait_ge(max_done.sem, max_done.at(r, j, per_half * u + 2))
                        ins = v.scalar_tensor_tensor(
                            out=dst, in0=heads, scalar=scale,
                            in1=scaled_max[:, u, :].unsqueeze(2).to_broadcast([P, 8, LEN]),
                            op0=ALU.mult, op1=ALU.subtract)
                    else:
                        ins = v.tensor_tensor(dst, heads, row_max[:, u, :].unsqueeze(2)
                                              .to_broadcast([P, 8, LEN]), ALU.subtract)
                    ins.then_inc(shifted_ready.sem, 1)

                def normalise(r, j):
                    dve.wait_ge(pv_t_ready.sem, pv_t_ready.at(r, j))
                    view = ps_post[:, 256:512].rearrange("p (h w e d) -> p h w e d", w=2, e=2, d=HD)
                    v.reciprocal(recip[:, :].rearrange("p (h e) -> p h e", e=2),
                                 view[:, :, 1, :, 0]).then_inc(recip_done.sem, 1)
                    dve.wait_ge(recip_done.sem, recip_done.at(r, j))
                    v.tensor_tensor(attn[:, :].rearrange("p (h e d) -> p h e d", e=2, d=HD), view[:, :, 0, :, :],
                                    recip[:, :].rearrange("p (h e) -> p h e", e=2).unsqueeze(3)
                                    .to_broadcast([P, HEADS // 2, 2, HD]), ALU.mult).then_inc(attn_ready.sem, 1)

                def residual(r, j):
                    layer, s = layer_of(j), j % STREAMS
                    dve.wait_ge(y_ready.sem, y_ready.at(r, j))
                    dve.wait_ge(x_bias_ready.sem, x_bias_ready.at(r, j))
                    if layer == L0_SELF:
                        dve.wait_ge(stored[s].sem, r * 16 + 16 * (j // PER_ROUND) + STORED_0)
                    after = post_steps if layer in POST_NORM else x_ready
                    v.tensor_tensor(x[:, s, :], ps_post[:, P:2 * P], x_bias[:, s, :],
                                    ALU.add).then_inc(after.sem, 1)
                    if layer in POST_NORM:
                        post_norm_begin(r, j, post_norm, POST_NORM[layer])

                def residual_end(r, j):
                    if layer_of(j) in POST_NORM:
                        post_norm_end(r, j, post_norm, POST_NORM[layer_of(j)], x_ready)

                def mlp_residual(r, j):
                    layer, s = layer_of(j), j % STREAMS
                    dve.wait_ge(mlp_y_ready.sem, mlp_y_ready.at(r, j))
                    dve.wait_ge(mlp_x_bias_ready.sem, mlp_x_bias_ready.at(r, j))
                    after = mlp_post_steps if layer in MLP_POST_NORM else mlp_x_ready
                    v.tensor_tensor(x[:, s, :], ps_k[:, 256:384], x_bias[:, s, :],
                                    ALU.add).then_inc(after.sem, 1)
                    if layer in MLP_POST_NORM:
                        post_norm_begin(r, j, mlp_post_norm, MLP_POST_NORM[layer])

                def mlp_residual_end(r, j):
                    if layer_of(j) in MLP_POST_NORM:
                        post_norm_end(r, j, mlp_post_norm, MLP_POST_NORM[layer_of(j)], mlp_x_ready)

                def phase(r, j):
                    core, post, pre = exists(r, j), exists(r, j - 1), exists(r, j + 1)
                    up, down, odd = has_mlp(r, j - UP), has_mlp(r, j - DOWN), (j - UP) % 2 == 1
                    if pre:
                        pre_norm_begin(r, j + 1)
                    if up:
                        mlp_norm_begin(r, j - UP)
                    if pre:
                        pre_norm_end(r, j + 1)
                    if up:
                        mlp_norm_end(r, j - UP)
                    if core:
                        shift(r, j, 0)
                    if post:
                        normalise(r, j - 1)
                    if core:
                        shift(r, j, 1)
                    if down:
                        mlp_residual(r, j - DOWN)
                    if pre:
                        pre_k(r, j + 1)
                    if post:
                        residual(r, j - 1)
                    if down:
                        mlp_residual_end(r, j - DOWN)
                    if post:
                        residual_end(r, j - 1)

                rounds(dve, phase)


SETUP_RAW_T = 8
SETUP_WIDE = SETUP_RAW_T + 9 + 11 + 5 + 3
SETUP_DVE = SETUP_WIDE + 4 + 4 + 6 + 3


def constants():
    c = np.arange(P)
    half = HD // 2
    inv_freq = (np.float32(1.0) / np.float32(10000.0) ** (np.arange(half, dtype=np.float32) / np.float32(half))).astype(np.float32)
    angle = (np.arange(LEN, dtype=np.float32)[None, :] * inv_freq[(c % half)][:, None]).astype(np.float32)
    return {
        "c_ident": np.eye(P, dtype=np.float32),
        "c_slot": ((c[:, None] // HD) % SLOTS == np.arange(SLOTS)[None, :]).astype(np.float32),
        "c_causal": ((c[:, None] % LEN) >= np.arange(LEN)[None, :]).astype(np.float32),
        "c_cos": np.cos(angle).astype(np.float32),
        "c_sin": np.sin(angle).astype(np.float32),
    }


def kernel(**inputs):
    import concourse.bacc as bacc
    from concourse.bass_utils import run_bass_kernel_spmd

    nc = bacc.Bacc("TRN2", target_bir_lowering=False, num_devices=1)
    arrays, aps = {}, {}
    for name, value in {**inputs, **constants()}.items():
        value = np.ascontiguousarray(value)
        arrays[f"in_{name}"] = value
        aps[name] = nc.dram_tensor(f"in_{name}", value.shape, mybir.dt.from_np(value.dtype),
                                   kind="ExternalInput").ap()
    out = nc.dram_tensor("out_0", (SEQS, LEN, DIM), F32, kind="ExternalOutput").ap()
    build(nc, aps, out)
    result = run_bass_kernel_spmd(nc, [arrays], core_ids=[0])
    return result.results[0]["out_0"]
```

```python
from contextlib import ExitStack

import numpy as np

import concourse.bass as bass
from concourse import mybir

F32 = mybir.dt.float32
BF16 = mybir.dt.bfloat16
I32 = mybir.dt.int32
ALU = mybir.AluOpType
ACT = mybir.ActivationFunctionType
AX_X = mybir.AxisListType.X

P = 128
SEQS, LEN, DIM = 128, 64, 128
HEADS, HD = 16, 8
HID = 512
PAIRS = SEQS * LEN // P
STREAMS = 8
ROUNDS = PAIRS // STREAMS
LAYERS = 7
PER_ROUND = LAYERS * STREAMS
QUADS, SLOTS = 4, 4
HALVES = 2
HCH = HID // P
PRE = 2
UP, DOWN = 3, 5
SCALE = float(HD) ** -0.5
MASKED = -1e30

L0_SELF, L0_CROSS, L1_CROSS, L2_SELF, L2_CROSS, L3_SELF, L3_CROSS = range(LAYERS)
CROSS = {L0_CROSS, L1_CROSS, L2_CROSS, L3_CROSS}
PRE_NORM = {L0_SELF: 1e-5, L0_CROSS: 1e-5, L1_CROSS: 1e-6, L3_SELF: 1e-6, L3_CROSS: 1e-6}
POST_NORM = {L2_SELF: (0, 1e-5), L2_CROSS: (1, 1e-5)}
MLP = {L0_CROSS: 0, L2_CROSS: 1, L3_CROSS: 2}
MLP_PRE_NORM = {L0_CROSS: 1e-5, L3_CROSS: 1e-6}
MLP_POST_NORM = {L2_CROSS: (2, 1e-6)}
GELU = {L0_CROSS: ACT.Gelu, L2_CROSS: ACT.Gelu, L3_CROSS: ACT.Gelu_apprx_tanh}
Q_BIAS = {L0_SELF, L0_CROSS, L3_SELF, L3_CROSS}
K_BIAS = {L0_SELF, L3_SELF, L3_CROSS}
MASK = {L0_SELF: 0, L2_SELF: 1, L2_CROSS: 2}
ROW_SCALE = {L2_SELF: 0, L2_CROSS: 1}


def layer_of(j):
    return (j % PER_ROUND) // STREAMS


class Norm:

    def __init__(self, sb, name, steps, root):
        self.stats = sb(f"{name}_stats", [P, 2, 6])
        self.mean_var = sb(f"{name}_mean_var", [P, 2, 2])
        self.mean_sq = sb(f"{name}_mean_sq", [P, 2])
        self.var_eps = sb(f"{name}_var_eps", [P, 2])
        self.rstd = sb(f"{name}_rstd", [P, 2])
        self.normed = sb(f"{name}_normed", [P, 2, DIM])
        self.steps, self.root = steps, root


class Signal:

    def __init__(self, sem, per_layer):
        self.sem = sem
        self.per_layer = [per_layer.get(layer, 0) if isinstance(per_layer, dict) else per_layer
                          for layer in range(LAYERS)]
        self.round = STREAMS * sum(self.per_layer)

    def at(self, r, j, m=None):
        full, rest = divmod(j, PER_ROUND)
        before = full * self.round + sum(self.per_layer[layer_of(i)] for i in range(rest))
        return r * self.round + (before + (self.per_layer[layer_of(j)] if m is None else m))


def build(nc, a, out):
    ctx = ExitStack()
    with ctx:
        def sb(name, shape, dt=F32):
            return ctx.enter_context(nc.sbuf_tensor(name, shape, dt))

        def sem(name):
            return ctx.enter_context(nc.semaphore(name))

        def signal(name, per_layer=1):
            return Signal(sem(name), per_layer)

        ident = sb("ident", [P, P])
        ident_bf = sb("ident_bf", [P, P], BF16)
        slot_mask = sb("slot_mask", [P, SLOTS])
        causal = sb("causal", [P, LEN])
        rope_cos = sb("rope_cos", [P, LEN])
        rope_sin = sb("rope_sin", [P, LEN])
        w_q = sb("w_q", [P, LAYERS, DIM])
        w_k = sb("w_k", [P, LAYERS, DIM])
        w_v = sb("w_v", [P, LAYERS, DIM])
        w_o = sb("w_o", [P, LAYERS, DIM])
        w_q_rot = sb("w_q_rot", [P, DIM])
        w_k_rot = sb("w_k_rot", [P, DIM])
        w_1 = sb("w_1", [P, len(MLP), HID])
        w_2 = sb("w_2", [P, len(MLP), HCH, DIM])
        b_q = sb("b_q", [P, LAYERS])
        b_k = sb("b_k", [P, LAYERS])
        b_v = sb("b_v", [P, LAYERS])
        b_1 = sb("b_1", [P, len(MLP), HCH])
        b_o_rows = sb("b_o_rows", [P, LAYERS, DIM])
        b_2_rows = sb("b_2_rows", [P, len(MLP), DIM])
        post_g = sb("post_g", [P, 3, DIM])
        post_b = sb("post_b", [P, 3, DIM])
        mask_int = sb("mask_int", [P, LEN], I32)
        mask_f = sb("mask_f", [P, LEN])
        mask_bias = sb("mask_bias", [P, 3, LEN], BF16)
        row_scale = sb("row_scale", [P, 2])
        raw = sb("raw", [P, 20, DIM])
        raw_t = sb("raw_t", [P, 8, DIM])
        vecs = sb("vecs", [P, 8])
        b_v_wide = sb("b_v_wide", [P, 3, P])
        valid = sb("valid", [P, LEN])

        x_in = sb("x_in", [P, STREAMS, DIM])
        ctx_in = sb("ctx_in", [P, STREAMS, DIM])
        x = sb("x", [P, STREAMS, DIM])
        x_bias = sb("x_bias", [P, STREAMS, DIM])
        ctx_t = sb("ctx_t", [P, STREAMS, 2, 2, LEN])
        q_quads = sb("q_quads", [P, STREAMS, QUADS, P])
        k_slots = sb("k_slots", [P, STREAMS, SLOTS, P])
        v_ones = sb("v_ones", [P, STREAMS, 2, HEADS // 2, 32])
        row_max = sb("row_max", [P, HALVES, 8])
        scaled_max = sb("scaled_max", [P, HALVES, 8])
        shifted = sb("shifted", [P, HALVES, 512])
        probs = sb("probs", [P, HALVES, 4, P])
        pv_sb = sb("pv_sb", [P, HALVES, P])
        recip = sb("recip", [P, HEADS])
        attn = sb("attn", [P, DIM])
        attn_t = sb("attn_t", [P, P])
        minus_half = sb("minus_half", [P, 1])
        h_t = sb("h_t", [P, 2, 2, LEN])
        mlp_h_t = sb("mlp_h_t", [P, P])
        gelu = sb("gelu", [P, 2, HCH, P])
        rope_a = sb("rope_a", [P, 2, P])
        rope_b = sb("rope_b", [P, 2, P])
        rope_qk = sb("rope_qk", [P, 2, P])

        def bank(name):
            return ctx.enter_context(nc.psum_tensor(name, [P, 512], F32))

        ps_scores = [bank("ps_scores0"), bank("ps_scores1")]
        ps_scores_t = bank("ps_scores_t")
        ps_post = bank("ps_post")
        ps_pre = bank("ps_pre")
        ps_q = bank("ps_q")
        ps_k = bank("ps_k")
        ps_hidden = [bank("ps_hidden"), ps_q]

        first_in = sem("first_in")
        first_in_pool = sem("first_in_pool")
        consts_in_pool = sem("consts_in_pool")
        consts_in = sem("consts_in")
        setup_mem = sem("setup_mem")
        setup_pe = sem("setup_pe")
        setup_dve = sem("setup_dve")
        first = {L0_SELF: 1}
        x_loaded = [signal(f"x_loaded{s}") for s in range(STREAMS)]
        ctx_loaded = [signal(f"ctx_loaded{s}") for s in range(STREAMS)]
        stored = [signal(f"stored{s}") for s in range(STREAMS)]
        scores_ready = signal("scores_ready", HALVES)
        scores_t_ready = signal("scores_t_ready", HALVES)
        pv_ready = signal("pv_ready")
        pv_t_ready = signal("pv_t_ready")
        attn_t_ready = signal("attn_t_ready")
        y_ready = signal("y_ready")
        mlp_t_ready = signal("mlp_t_ready", {n: 1 for n in MLP})
        hidden_ready = signal("hidden_ready", {n: 1 for n in MLP})
        mlp_y_ready = signal("mlp_y_ready", {n: 1 for n in MLP})
        h_t_ready = signal("h_t_ready")
        ctx_t_ready = signal("ctx_t_ready", first)
        q_ready = signal("q_ready")
        k_ready = signal("k_ready")
        v_ready = signal("v_ready")
        max_done = signal("max_done", {n: 4 if n in ROW_SCALE else 2 for n in range(LAYERS)})
        shifted_ready = signal("shifted_ready", HALVES)
        recip_done = signal("recip_done")
        attn_ready = signal("attn_ready")
        x_ready = signal("x_ready", {n: 1 for n in range(LAYERS) if n not in POST_NORM})
        post_steps = signal("post_steps", {n: 3 for n in POST_NORM})
        mlp_steps = signal("mlp_steps", {n: 2 for n in MLP_PRE_NORM})
        mlp_x_ready = signal("mlp_x_ready", {n: 1 for n in MLP if n not in MLP_POST_NORM})
        mlp_post_steps = signal("mlp_post_steps", {n: 3 for n in MLP_POST_NORM})
        pre_steps = signal("pre_steps", {n: 3 if n == L1_CROSS else 2 for n in PRE_NORM})
        rope_steps = signal("rope_steps", {L1_CROSS: 4})
        rope_ready = signal("rope_ready", {L1_CROSS: 1})
        k_slots_ready = signal("k_slots_ready")
        probs_ready = signal("probs_ready", HALVES)
        pv_copied = signal("pv_copied")
        attn_t_copied = signal("attn_t_copied")
        mlp_t_copied = signal("mlp_t_copied", {n: 1 for n in MLP})
        gelu_ready = signal("gelu_ready", {n: 1 for n in MLP})
        h_t_copied = signal("h_t_copied")
        ctx_t_copied = signal("ctx_t_copied", first)
        q_quads_ready = signal("q_quads_ready")
        v_ready_sb = signal("v_ready_sb")
        post_rstd = signal("post_rstd", {n: 4 for n in POST_NORM})
        mlp_rstd = signal("mlp_rstd", {n: 2 for n in MLP_PRE_NORM})
        mlp_post_rstd = signal("mlp_post_rstd", {n: 4 for n in MLP_POST_NORM})
        post_x_ready = signal("post_x_ready", {n: 1 for n in POST_NORM})
        mlp_post_x_ready = signal("mlp_post_x_ready", {n: 1 for n in MLP_POST_NORM})
        h_ready = signal("h_ready", {n: 1 for n in PRE_NORM})
        mlp_h_ready = signal("mlp_h_ready", {n: 1 for n in MLP_PRE_NORM})
        pre_rstd = signal("pre_rstd", {n: 1 if n == L1_CROSS else 2 for n in PRE_NORM})
        pre_norm = Norm(sb, "pre", pre_steps, pre_rstd)
        mlp_norm = Norm(sb, "mlp", mlp_steps, mlp_rstd)
        post_norm = Norm(sb, "post", post_steps, post_rstd)
        mlp_post_norm = Norm(sb, "mlp_post", mlp_post_steps, mlp_post_rstd)
        x_bias_ready = signal("x_bias_ready")
        mlp_x_bias_ready = signal("mlp_x_bias_ready", {n: 1 for n in MLP})

        x_dram = a["x"].rearrange("(n two) t c -> n (two t) c", two=2)
        ctx_dram = a["ctx_1024"].rearrange("(n two) t c -> n (two t) c", two=2)
        out_dram = out.rearrange("(n two) t c -> n (two t) c", two=2)

        def rounds(eng, phase):
            for j in range(-PRE - 1, STREAMS - 1):
                phase(0, j)
            with eng.Fori(0, ROUNDS - 1) as r:
                for j in range(STREAMS - 1, STREAMS - 1 + PER_ROUND):
                    phase(r, j)
            for j in range(STREAMS - 1, PER_ROUND + STREAMS - 1):
                phase(ROUNDS - 1, j)

        def exists(r, j):
            return not isinstance(r, int) or 0 <= PER_ROUND * r + j < PER_ROUND * ROUNDS

        def latest(r, j):
            return min(j, PER_ROUND * (ROUNDS - r) - 1) if isinstance(r, int) else j

        def has_mlp(r, j):
            return exists(r, j) and layer_of(j) in MLP

        def pre_source(j):
            return (x_in if layer_of(j) == L0_SELF else x)[:, j % STREAMS, :]

        def load_count(r, j):
            return r * 16 + (16 * (j // PER_ROUND) + 16)

        def first_round(r, j):
            return isinstance(r, int) and PER_ROUND * r + j < STREAMS

        def residual_read(r, j):
            if layer_of(j) in POST_NORM:
                return post_steps.sem, post_steps.at(r, j, 1)
            return x_ready.sem, x_ready.at(r, j)

        def mlp_residual_read(r, j):
            if layer_of(j) in MLP_POST_NORM:
                return mlp_post_steps.sem, mlp_post_steps.at(r, j, 1)
            return mlp_x_ready.sem, mlp_x_ready.at(r, j)

        def last_x_signal(layer):
            if layer in MLP:
                return mlp_post_x_ready if layer in MLP_POST_NORM else mlp_x_ready
            return attention_x_signal(layer)

        def attention_x_signal(layer):
            return post_x_ready if layer in POST_NORM else x_ready

        def col(name, lo=0):
            return a[name][lo:lo + P].unsqueeze(1)

        def row(name):
            return a[name].unsqueeze(0).to_broadcast([P, DIM])

        def chunks(name, n):
            return a[name].rearrange("(n p) c -> p n c", p=P) if n > 1 else a[name]

        loads = [
            (ident[:, :], a["c_ident"]),
            (raw[:, 0:3, :], chunks("L0_xattn_w_qkv", 3)), (raw[:, 3, :], a["L0_xattn_w_q"]),
            (raw[:, 4:8, :], chunks("L0_xattn_w_fc1", 4)), (raw[:, 8, :], a["L1_xattn_Wq"]),
            (raw[:, 9, :], a["L0_xattn_w_prj1"]), (raw[:, 10, :], a["L0_xattn_w_prj2"]),
            (raw[:, 11:13, :], chunks("L0_xattn_w_kv", 2)), (raw[:, 13:15, :], chunks("L1_xattn_Wkv", 2)),
            (raw[:, 15, :], a["L1_xattn_Wo"]),
            (raw[:, 16:20, :], a["L0_xattn_w_fc2"].rearrange("p (n c) -> p n c", c=P)),
            (vecs[:, 0:1], col("L0_xattn_ln1_g")), (vecs[:, 1:2], col("L0_xattn_ln1_b")),
            (vecs[:, 2:3], col("L0_xattn_ln2_g")), (vecs[:, 3:4], col("L0_xattn_ln2_b")),
            (vecs[:, 4:5], col("L0_xattn_ln3_g")), (vecs[:, 5:6], col("L0_xattn_ln3_b")),
            (vecs[:, 6:7], col("L1_xattn_norm_w")),
        ]
        N_FIRST = len(loads)
        loads += [
            (slot_mask[:, :], a["c_slot"]), (causal[:, :], a["c_causal"]),
            (rope_cos[:, :], a["c_cos"]), (rope_sin[:, :], a["c_sin"]),
            (w_q[:, 3, :], a["L2_xattn_Wqkv"][:, 0:128]), (w_k[:, 3, :], a["L2_xattn_Wqkv"][:, 128:256]),
            (w_v[:, 3, :], a["L2_xattn_Wqkv"][:, 256:384]), (w_o[:, 3, :], a["L2_xattn_Wo1"]),
            (w_q[:, 4, :], a["L2_xattn_Wq"]), (w_k[:, 4, :], a["L2_xattn_Wk"]),
            (w_v[:, 4, :], a["L2_xattn_Wv"]), (w_o[:, 4, :], a["L2_xattn_Wo2"]),
            (w_q[:, 5, :], a["L3_xattn_Wqkv"][:, 0:128]), (w_k[:, 5, :], a["L3_xattn_Wqkv"][:, 128:256]),
            (w_v[:, 5, :], a["L3_xattn_Wqkv"][:, 256:384]), (w_o[:, 5, :], a["L3_xattn_Wos"]),
            (w_q[:, 6, :], a["L3_xattn_Wq"]), (w_k[:, 6, :], a["L3_xattn_Wkv"][:, 0:128]),
            (w_v[:, 6, :], a["L3_xattn_Wkv"][:, 128:256]), (w_o[:, 6, :], a["L3_xattn_Woc"]),
            (w_1[:, 1, :], a["L2_xattn_W1"]), (w_1[:, 2, :], a["L3_xattn_W1"]),
            (w_2[:, 1, :, :], chunks("L2_xattn_W2", 4)), (w_2[:, 2, :, :], chunks("L3_xattn_W2", 4)),
            (b_q[:, 5:6], col("L3_xattn_bqkv")), (b_k[:, 5:6], col("L3_xattn_bqkv", 128)),
            (b_v[:, 5:6], col("L3_xattn_bqkv", 256)), (b_q[:, 6:7], col("L3_xattn_bq")),
            (b_k[:, 6:7], col("L3_xattn_bkv")), (b_v[:, 6:7], col("L3_xattn_bkv", 128)),
            (b_o_rows[:, 0, :], row("L0_xattn_b_prj1")), (b_o_rows[:, 1, :], row("L0_xattn_b_prj2")),
            (b_o_rows[:, 3, :], row("L2_xattn_bo1")), (b_o_rows[:, 4, :], row("L2_xattn_bo2")),
            (b_o_rows[:, 5, :], row("L3_xattn_bos")), (b_o_rows[:, 6, :], row("L3_xattn_boc")),
            (b_2_rows[:, 0, :], row("L0_xattn_b_fc2")), (b_2_rows[:, 1, :], row("L2_xattn_bf2")),
            (b_2_rows[:, 2, :], row("L3_xattn_b2")),
            (post_g[:, 0, :], row("L2_xattn_g1")), (post_g[:, 1, :], row("L2_xattn_g2")),
            (post_g[:, 2, :], row("L2_xattn_g3")), (post_b[:, 0, :], row("L2_xattn_b1")),
            (post_b[:, 1, :], row("L2_xattn_b2")), (post_b[:, 2, :], row("L2_xattn_b3")),
            (mask_int[:, :], a["mask_1xS2_if1"].to_broadcast([P, LEN])),
        ]
        for m, name in enumerate(("L0_xattn_b_fc1", "L2_xattn_bf1", "L3_xattn_b1")):
            for c in range(HCH):
                loads.append((b_1[:, m, c:c + 1], col(name, c * P)))
        N_LOADS = len(loads)

        def load_constants(eng, which):
            for n in range(which, N_LOADS, 3):
                done = (first_in_pool if n < N_FIRST else consts_in_pool) if which == 2 else \
                       (first_in if n < N_FIRST else consts_in)
                eng.dma_start(*loads[n]).then_inc(done, 16)

        pool_first, pool_all = len(range(2, N_FIRST, 3)), len(range(2, N_LOADS, 3))

        def wait_first_loads(eng):
            eng.wait_ge(first_in, 16 * (N_FIRST - pool_first))
            eng.wait_ge(first_in_pool, 16 * pool_first)

        def wait_other_loads(eng):
            eng.wait_ge(consts_in, 16 * (N_LOADS - N_FIRST - (pool_all - pool_first)))
            eng.wait_ge(consts_in_pool, 16 * (pool_all - pool_first))

        scaled_to = [(w_q[:, 0, :], 0), (w_k[:, 0, :], 0), (w_v[:, 0, :], 0), (w_q[:, 1, :], 2)] + \
                    [(w_1[:, 0, c * P:(c + 1) * P], 4) for c in range(HCH)] + [(w_q[:, 2, :], 6)]
        copied_to = [w_o[:, 0, :], w_o[:, 1, :], w_k[:, 1, :], w_v[:, 1, :], w_k[:, 2, :], w_v[:, 2, :],
                     w_o[:, 2, :]] + [w_2[:, 0, c, :] for c in range(HCH)]
        setup_banks = [ps_scores[0], ps_scores[1], ps_scores_t, ps_post, ps_pre]

        def setup_psum(n):
            return setup_banks[n // 4][:, (n % 4) * P:(n % 4 + 1) * P]

        N_MEM = 8
        STORED_0 = 1

        with nc.Block() as block:

            @block.sync
            def _(sp):
                load_constants(sp, 0)

                def load(n, s):
                    sp.dma_start(x_in[:, s, :], x_dram[bass.ds(n, 1), :, :].rearrange("n p c -> (n p) c")
                                 if not isinstance(n, int) else x_dram[n]).then_inc(x_loaded[s].sem, 16)
                    sp.dma_start(ctx_in[:, s, :], ctx_dram[bass.ds(n, 1), :, :].rearrange("n p c -> (n p) c")
                                 if not isinstance(n, int) else ctx_dram[n]).then_inc(ctx_loaded[s].sem, 16)

                def store(r, n, s):
                    sp.wait_ge(mlp_x_ready.sem, mlp_x_ready.at(r, PER_ROUND - STREAMS + s))
                    sp.dma_start(out_dram[bass.ds(n, 1), :, :].rearrange("n p c -> (n p) c")
                                 if not isinstance(n, int) else out_dram[n], x[:, s, :]).then_inc(stored[s].sem, 16)

                for s in range(STREAMS):
                    load(s, s)
                with sp.Fori(0, ROUNDS - 1) as r:
                    pair = [sp.snap(STREAMS * r + k) for k in range(2 * STREAMS)]
                    sp.wait_ge(h_ready.sem, h_ready.at(r, STREAMS - 1))
                    sp.wait_ge(x_bias_ready.sem, x_bias_ready.at(r, STREAMS - 1))
                    sp.wait_ge(ctx_t_ready.sem, ctx_t_ready.at(r, STREAMS - 1))
                    for s in range(STREAMS):
                        load(pair[STREAMS + s], s)
                    for s in range(STREAMS):
                        store(r, pair[s], s)
                for s in range(STREAMS):
                    store(ROUNDS - 1, PAIRS - STREAMS + s, s)
                for s in range(STREAMS):
                    sp.wait_ge(stored[s].sem, 16 * ROUNDS + STORED_0)

            @block.gpsimd
            def _(pool):
                load_constants(pool, 2)
                pool.memset(v_ones[:, :, :, :, 0:16], 0.0).then_inc(setup_mem, 1)
                pool.memset(b_o_rows[:, L1_CROSS, :], 0.0).then_inc(setup_mem, 1)
                pool.memset(minus_half[:, :], -0.5).then_inc(setup_mem, 1)
                wait_other_loads(pool)
                pool.wait_ge(setup_dve, SETUP_DVE)

                def inverse_root(r, j, norm, m=None):
                    b = j % 2
                    pool.wait_ge(norm.steps.sem, norm.steps.at(r, j, m))
                    pool.tensor_tensor(norm.rstd[:, b:b + 1], norm.var_eps[:, b:b + 1], minus_half[:, :],
                                       ALU.pow).then_inc(norm.root.sem, 1)

                def normalised(r, j, norm, src, rms=False):
                    b = j % 2
                    if not rms:
                        pool.tensor_tensor(norm.normed[:, b, :], src, norm.mean_var[:, b, 0:1]
                                           .to_broadcast([P, DIM]), ALU.subtract).then_inc(norm.root.sem, 1)
                        src = norm.normed[:, b, :]
                    pool.wait_ge(norm.root.sem, norm.root.at(r, j, 1 if rms else 2))
                    return pool.tensor_tensor(norm.normed[:, b, :], src, norm.rstd[:, b:b + 1]
                                              .to_broadcast([P, DIM]), ALU.mult)

                def pre_norm_end(r, j):
                    layer = layer_of(j)
                    if layer in PRE_NORM:
                        inverse_root(r, j, pre_norm)
                        normalised(r, j, pre_norm, pre_source(j), rms=layer == L1_CROSS) \
                            .then_inc(h_ready.sem, 1)

                def mlp_norm_end(r, j):
                    if layer_of(j) in MLP_PRE_NORM:
                        inverse_root(r, j, mlp_norm)
                        normalised(r, j, mlp_norm, x[:, j % STREAMS, :]).then_inc(mlp_h_ready.sem, 1)

                def post_norm_end(r, j, norm, which, ready):
                    s, g, b = j % STREAMS, which[0], j % 2
                    inverse_root(r, j, norm, 3)
                    normalised(r, j, norm, x[:, s, :]).then_inc(norm.root.sem, 1)
                    pool.wait_ge(norm.root.sem, norm.root.at(r, j, 3))
                    pool.tensor_tensor(norm.normed[:, b, :], norm.normed[:, b, :], post_g[:, g, :],
                                       ALU.mult).then_inc(norm.root.sem, 1)
                    pool.wait_ge(norm.root.sem, norm.root.at(r, j, 4))
                    pool.tensor_tensor(x[:, s, :], norm.normed[:, b, :], post_b[:, g, :],
                                       ALU.add).then_inc(ready.sem, 1)

                def residual_end(r, j):
                    if layer_of(j) in POST_NORM:
                        post_norm_end(r, j, post_norm, POST_NORM[layer_of(j)], post_x_ready)

                def mlp_residual_end(r, j):
                    if layer_of(j) in MLP_POST_NORM:
                        post_norm_end(r, j, mlp_post_norm, MLP_POST_NORM[layer_of(j)], mlp_post_x_ready)

                def attention_bias(r, j):
                    layer, s = layer_of(j), j % STREAMS
                    if layer == L0_SELF:
                        pool.wait_ge(x_loaded[s].sem, load_count(r, j))
                        src = x_in
                        if not first_round(r, j):
                            pool.wait_ge(mlp_x_ready.sem, mlp_x_ready.at(r, j - STREAMS))
                    else:
                        done = last_x_signal(layer_of(j - STREAMS))
                        pool.wait_ge(done.sem, done.at(r, j - STREAMS))
                        src = x
                    pool.tensor_tensor(x_bias[:, s, :], src[:, s, :], b_o_rows[:, layer, :],
                                       ALU.add).then_inc(x_bias_ready.sem, 1)

                def mlp_bias(r, j):
                    layer, s = layer_of(j), j % STREAMS
                    done = attention_x_signal(layer)
                    pool.wait_ge(done.sem, done.at(r, j))
                    pool.tensor_tensor(x_bias[:, s, :], x[:, s, :], b_2_rows[:, MLP[layer], :],
                                       ALU.add).then_inc(mlp_x_bias_ready.sem, 1)

                def phase(r, j):
                    post = exists(r, j - 1)
                    up, down = has_mlp(r, j - UP), has_mlp(r, j - DOWN)
                    if down:
                        mlp_residual_end(r, j - DOWN)
                    if post:
                        residual_end(r, j - 1)
                    if up:
                        mlp_bias(r, j - UP)
                    if exists(r, j + 1):
                        attention_bias(r, j + 1)
                    if has_mlp(r, j - UP + 1):
                        mlp_norm_end(r, j - UP + 1)
                    if exists(r, j + PRE + 1):
                        pre_norm_end(r, j + PRE + 1)

                rounds(pool, phase)

            @block.scalar
            def _(act):
                load_constants(act, 1)
                wait_other_loads(act)
                act.wait_ge(setup_mem, N_MEM)
                act.wait_ge(setup_dve, SETUP_DVE)

                def copy_h_t(r, j):
                    act.wait_ge(h_t_ready.sem, h_t_ready.at(r, j))
                    nc.scalar.copy(h_t[:, :, :, :], ps_pre[:, P:2 * P].rearrange("p (b t) -> p b t", b=2)
                                   .unsqueeze(2).to_broadcast([P, 2, 2, LEN])).then_inc(h_t_copied.sem, 1)
                    if layer_of(j) == L0_SELF:
                        act.wait_ge(ctx_t_ready.sem, ctx_t_ready.at(r, j))
                        nc.scalar.copy(ctx_t[:, j % STREAMS, :, :, :], ps_pre[:, 0:P]
                                       .rearrange("p (b t) -> p b t", b=2).unsqueeze(2)
                                       .to_broadcast([P, 2, 2, LEN])).then_inc(ctx_t_copied.sem, 1)

                def copy_q(r, j):
                    layer, s = layer_of(j), j % STREAMS
                    if layer == L1_CROSS:
                        act.wait_ge(rope_ready.sem, rope_ready.at(r, j))
                        src = rope_qk[:, 0, :]
                    else:
                        act.wait_ge(q_ready.sem, q_ready.at(r, j))
                        src = ps_q[:, 0:P]
                    for g in range(QUADS):
                        rows = slice(32 * g, 32 * g + 32)
                        if layer in Q_BIAS:
                            ins = nc.scalar.activation(q_quads[rows, s, g, :], src[rows, :], ACT.Identity,
                                                       bias=b_q[rows, layer:layer + 1])
                        else:
                            ins = nc.scalar.copy(q_quads[rows, s, g, :], src[rows, :])
                    ins.then_inc(q_quads_ready.sem, 1)

                def copy_v(r, j):
                    s = j % STREAMS
                    act.wait_ge(v_ready.sem, v_ready.at(r, j))
                    for e in range(2):
                        rows = slice(64 * e, 64 * e + 64)
                        ins = nc.scalar.copy(
                            v_ones[rows, s, :, :, HD * e:HD * e + HD].rearrange("p b h d -> p (b h) d"),
                            ps_pre[rows, 256:512].rearrange("p (bh e d) -> p bh e d", e=2, d=HD)[:, :, e, :])
                    ins.then_inc(v_ready_sb.sem, 1)

                def copy_pv(r, j):
                    act.wait_ge(pv_ready.sem, pv_ready.at(r, j))
                    nc.scalar.copy(pv_sb[:, :, :], ps_post[:, 0:256].rearrange("p (u t) -> p u t", u=2)) \
                        .then_inc(pv_copied.sem, 1)

                def copy_attn_t(r, j):
                    act.wait_ge(attn_t_ready.sem, attn_t_ready.at(r, j))
                    nc.scalar.copy(attn_t[:, :], ps_post[:, 0:P]).then_inc(attn_t_copied.sem, 1)

                def copy_mlp_t(r, j):
                    act.wait_ge(mlp_t_ready.sem, mlp_t_ready.at(r, j))
                    nc.scalar.copy(mlp_h_t[:, :], ps_pre[:, 0:P]).then_inc(mlp_t_copied.sem, 1)

                def gelus(r, j):
                    layer = layer_of(j)
                    act.wait_ge(hidden_ready.sem, hidden_ready.at(r, j))
                    for c in range(HCH):
                        ins = nc.scalar.activation(gelu[:, j % 2, c, :], ps_hidden[j % 2][:, c * P:(c + 1) * P], GELU[layer],
                                                   bias=b_1[:, MLP[layer], c:c + 1])
                    ins.then_inc(gelu_ready.sem, 1)

                def exps(r, j, u):
                    act.wait_ge(scores_t_ready.sem, scores_t_ready.at(r, j, u + 1))
                    nc.scalar.activation(probs[:, u, :, :], ps_scores_t[:, :]
                                         .rearrange("p (h t) -> p h t", h=4), ACT.Exp,
                                         scale=SCALE).then_inc(probs_ready.sem, 1)

                def phase(r, j):
                    core, post, pre = exists(r, j), exists(r, j - 1), exists(r, j + PRE)
                    up, odd = has_mlp(r, j - UP), (j - UP) % 2 == 1
                    if post:
                        copy_pv(r, j - 1)
                    if (j - 1 - UP) % 2 == 1 and has_mlp(r, j - 1 - UP):
                        gelus(r, j - 1 - UP)
                    if up:
                        copy_mlp_t(r, j - UP)
                    if pre:
                        copy_h_t(r, j + PRE)
                    if core:
                        exps(r, j, 0)
                    if post:
                        copy_attn_t(r, j - 1)
                    if pre and layer_of(j + PRE) != L1_CROSS:
                        copy_q(r, j + PRE)
                    if pre:
                        copy_v(r, j + PRE)
                    if core:
                        exps(r, j, 1)
                    if pre and layer_of(j + PRE) == L1_CROSS:
                        copy_q(r, j + PRE)
                    if up and odd:
                        gelus(r, j - UP - 1)

                rounds(act, phase)

            @block.tensor
            def _(pe):
                wait_first_loads(pe)
                for n in range(20):
                    ins = nc.tensor.transpose(setup_psum(n), raw[:, n, :], ident[:, :])
                ins.then_inc(setup_pe, 1)
                pe.wait_ge(setup_dve, SETUP_RAW_T)
                for i, (n, vec) in enumerate(((0, 1), (1, 1), (2, 1), (3, 3), (4, 5), (5, 5), (6, 5), (7, 5))):
                    ins = nc.tensor.matmul(ps_q[:, i:i + 1], raw_t[:, n, :], vecs[:, vec:vec + 1],
                                           start=True, stop=True)
                ins.then_inc(setup_pe, 1)
                pe.wait_ge(setup_dve, SETUP_WIDE)
                for i, layer in enumerate((0, 5, 6)):
                    ins = nc.tensor.matmul(ps_k[:, i * P:(i + 1) * P], b_v_wide[:, i, :], w_o[:, layer, :],
                                           start=True, stop=True)
                ins.then_inc(setup_pe, 1)
                pe.wait_ge(setup_dve, SETUP_DVE)
                pe.wait_ge(setup_mem, N_MEM)

                def bank_pre_free(r, j):
                    if exists(r, j - 1):
                        pe.wait_ge(v_ready_sb.sem, v_ready_sb.at(r, j - 1))
                    if has_mlp(r, j - PRE - UP):
                        pe.wait_ge(mlp_t_copied.sem, mlp_t_copied.at(r, j - PRE - UP))

                def pre_h(r, j):
                    layer, s = layer_of(j), j % STREAMS
                    if layer in PRE_NORM:
                        pe.wait_ge(h_ready.sem, h_ready.at(r, j))
                        src = pre_norm.normed[:, j % 2, :]
                    else:
                        done = last_x_signal(layer_of(j - STREAMS))
                        pe.wait_ge(done.sem, done.at(r, j - STREAMS))
                        src = x[:, s, :]
                    bank_pre_free(r, j)
                    nc.tensor.transpose(ps_pre[:, P:2 * P], src, ident[:, :]).then_inc(h_t_ready.sem, 1)
                    if layer == L0_SELF:
                        pe.wait_ge(ctx_loaded[s].sem, load_count(r, j))
                        pe.wait_ge(h_t_copied.sem, h_t_copied.at(r, j))
                        nc.tensor.transpose(ps_pre[:, 0:P], ctx_in[:, s, :], ident[:, :]) \
                            .then_inc(ctx_t_ready.sem, 1)

                def pre_qk(r, j):
                    layer, s = layer_of(j), j % STREAMS
                    pe.wait_ge(h_t_copied.sem, h_t_copied.at(r, j))
                    tokens = h_t[:, :, 0, :]
                    kv_tokens = ctx_t[:, s, :, 0, :] if layer in CROSS else tokens
                    if (j - PRE - 1 - UP) % 2 == 1 and has_mlp(r, j - PRE - 1 - UP):
                        pe.wait_ge(gelu_ready.sem, gelu_ready.at(r, j - PRE - 1 - UP))
                    ins = nc.tensor.matmul(ps_q[:, 0:P], w_q[:, layer, :], tokens, start=True, stop=True)
                    if layer == L1_CROSS:
                        ins = nc.tensor.matmul(ps_q[:, P:2 * P], w_q_rot[:, :], tokens, start=True, stop=True)
                    ins.then_inc(q_ready.sem, 1)
                    if has_mlp(r, j - PRE - DOWN):
                        pe.wait_ge(*mlp_residual_read(r, j - PRE - DOWN))
                    ins = nc.tensor.matmul(ps_k[:, 0:P], w_k[:, layer, :], kv_tokens, start=True, stop=True)
                    if layer == L1_CROSS:
                        ins = nc.tensor.matmul(ps_k[:, P:2 * P], w_k_rot[:, :], kv_tokens, start=True, stop=True)
                    ins.then_inc(k_ready.sem, 1)

                def pre_v(r, j):
                    layer, s = layer_of(j), j % STREAMS
                    if layer == L0_SELF:
                        pe.wait_ge(ctx_t_copied.sem, ctx_t_copied.at(r, j))
                    for b in range(2):
                        src = ctx_t[:, s, b, :, :] if layer in CROSS else h_t[:, b, :, :]
                        ins = nc.tensor.matmul(ps_pre[:, 256 + b * P:256 + (b + 1) * P],
                                               src.rearrange("p k t -> p (k t)"), w_v[:, layer, :],
                                               start=True, stop=True)
                    ins.then_inc(v_ready.sem, 1)

                def scores(r, j, u):
                    layer, s = layer_of(j), j % STREAMS
                    if u == 0:
                        pe.wait_ge(q_quads_ready.sem, q_quads_ready.at(r, j))
                        pe.wait_ge(k_slots_ready.sem, k_slots_ready.at(r, j))
                    for g in (2 * u, 2 * u + 1):
                        cols = slice((g % 2) * 256, (g % 2) * 256 + 256)
                        for b in range(2):
                            ins = nc.tensor.matmul(ps_scores[u][64 * b:64 * b + 64, cols],
                                                   q_quads[:, s, g, 64 * b:64 * b + 64],
                                                   k_slots[:, s, :, 64 * b:64 * b + 64],
                                                   start=True, stop=layer not in MASK)
                        if layer in MASK:
                            for b in range(2):
                                ins = nc.tensor.matmul(ps_scores[u][64 * b:64 * b + 64, cols],
                                                       ident_bf[:, 64 * b:64 * b + 64],
                                                       mask_bias[:, MASK[layer], :].unsqueeze(1)
                                                       .to_broadcast([P, SLOTS, LEN]),
                                                       start=False, stop=True)
                    ins.then_inc(scores_ready.sem, 1)

                def transposes(r, j, u):
                    pe.wait_ge(shifted_ready.sem, shifted_ready.at(r, j, u + 1))
                    if u:
                        pe.wait_ge(probs_ready.sem, probs_ready.at(r, j, u))
                    for h in range(4):
                        ins = nc.tensor.transpose(ps_scores_t[:, h * P:(h + 1) * P],
                                                  shifted[:, u, h * P:(h + 1) * P], ident[:, :])
                    ins.then_inc(scores_t_ready.sem, 1)

                def values(r, j, u):
                    s = j % STREAMS
                    if u == 0:
                        pe.wait_ge(v_ready_sb.sem, v_ready_sb.at(r, j))
                        if exists(r, j - 1):
                            pe.wait_ge(*residual_read(r, j - 1))
                    pe.wait_ge(probs_ready.sem, probs_ready.at(r, j, u + 1))
                    for b in range(2):
                        for h in range(4):
                            ins = nc.tensor.matmul(ps_post[32 * h:32 * h + 32, u * P + 64 * b:u * P + 64 * b + 64],
                                                   v_ones[:, s, b, 4 * u + h, :],
                                                   probs[:, u, h, 64 * b:64 * b + 64], start=True, stop=True)
                    if u == HALVES - 1:
                        ins.then_inc(pv_ready.sem, 1)

                def pv_t(r, j):
                    pe.wait_ge(pv_copied.sem, pv_copied.at(r, j))
                    for u in range(HALVES):
                        ins = nc.tensor.transpose(ps_post[:, 256 + u * P:256 + (u + 1) * P], pv_sb[:, u, :],
                                                  ident[:, :])
                    ins.then_inc(pv_t_ready.sem, 1)

                def attn_turn(r, j):
                    pe.wait_ge(attn_ready.sem, attn_ready.at(r, j))
                    nc.tensor.transpose(ps_post[:, 0:P], attn[:, :], ident[:, :]) \
                        .then_inc(attn_t_ready.sem, 1)

                def project(r, j):
                    pe.wait_ge(attn_t_copied.sem, attn_t_copied.at(r, j))
                    nc.tensor.matmul(ps_post[:, P:2 * P], attn_t[:, :], w_o[:, layer_of(j), :],
                                     start=True, stop=True).then_inc(y_ready.sem, 1)

                def mlp_turn(r, j):
                    layer, s = layer_of(j), j % STREAMS
                    if layer in MLP_PRE_NORM:
                        pe.wait_ge(mlp_h_ready.sem, mlp_h_ready.at(r, j))
                        src = mlp_norm.normed[:, j % 2, :]
                    else:
                        done = attention_x_signal(layer)
                        pe.wait_ge(done.sem, done.at(r, j))
                        src = x[:, s, :]
                    last_v = latest(r, j + UP + PRE - 1)
                    pe.wait_ge(v_ready_sb.sem, v_ready_sb.at(r, last_v))
                    nc.tensor.transpose(ps_pre[:, 0:P], src, ident[:, :]).then_inc(mlp_t_ready.sem, 1)

                def mlp_up(r, j):
                    pe.wait_ge(mlp_t_copied.sem, mlp_t_copied.at(r, j))
                    if j % 2 == 1:
                        last_q = latest(r, j + UP + PRE)
                        q_read = rope_ready if layer_of(last_q) == L1_CROSS else q_quads_ready
                        pe.wait_ge(q_read.sem, q_read.at(r, last_q))
                    for c in range(HCH):
                        ins = nc.tensor.matmul(ps_hidden[j % 2][:, c * P:(c + 1) * P],
                                               w_1[:, MLP[layer_of(j)], c * P:(c + 1) * P], mlp_h_t[:, :],
                                               start=True, stop=True)
                    ins.then_inc(hidden_ready.sem, 1)

                def mlp_down(r, j):
                    pe.wait_ge(gelu_ready.sem, gelu_ready.at(r, j))
                    last_k = latest(r, j + DOWN + PRE - 1)
                    pe.wait_ge(k_slots_ready.sem, k_slots_ready.at(r, last_k))
                    if not exists(r, j + DOWN + PRE - 1) and has_mlp(r, j - 1):
                        pe.wait_ge(*mlp_residual_read(r, j - 1))
                    for c in range(HCH):
                        ins = nc.tensor.matmul(ps_k[:, 256:384], gelu[:, j % 2, c, :], w_2[:, MLP[layer_of(j)], c, :],
                                               start=c == 0, stop=c == HCH - 1)
                    ins.then_inc(mlp_y_ready.sem, 1)

                def phase(r, j):
                    core, post, pre = exists(r, j), exists(r, j - 1), exists(r, j + PRE)
                    up, down, odd = has_mlp(r, j - UP), has_mlp(r, j - DOWN), (j - UP) % 2 == 1
                    if core:
                        scores(r, j, 0)
                    if post:
                        values(r, j - 1, 0)
                        values(r, j - 1, 1)
                    if core:
                        scores(r, j, 1)
                    if up:
                        mlp_turn(r, j - UP)
                    if post:
                        pv_t(r, j - 1)
                    if core:
                        transposes(r, j, 0)
                    if down:
                        mlp_down(r, j - DOWN)
                    if pre:
                        pre_h(r, j + PRE)
                    if up and not odd:
                        mlp_up(r, j - UP)
                    if post:
                        attn_turn(r, j - 1)
                    if pre:
                        pre_qk(r, j + PRE)
                        pre_v(r, j + PRE)
                    if post:
                        project(r, j - 1)
                    if core:
                        transposes(r, j, 1)
                    if up and odd:
                        mlp_up(r, j - UP)

                rounds(pe, phase)

            @block.vector
            def _(dve):
                v = nc.vector
                v.memset(q_quads[:, :, :, :], 0.0).then_inc(setup_mem, 1)
                for rows, one, zero in ((slice(0, 64), 16, 24), (slice(64, 128), 24, 16)):
                    v.memset(v_ones[rows, :, :, :, one:one + HD], 1.0).then_inc(setup_mem, 1)
                    v.memset(v_ones[rows, :, :, :, zero:zero + HD], 0.0).then_inc(setup_mem, 1)
                wait_first_loads(dve)
                for s in range(STREAMS):
                    v.memset(x[:, s, 0:1], 0.0).then_inc(stored[s].sem, STORED_0)
                done = [0]

                def step(ins):
                    done[0] += 1
                    ins.then_inc(setup_dve, 1)

                def settle():
                    dve.wait_ge(setup_dve, done[0])

                dve.wait_ge(setup_pe, 1)
                for n in range(8):
                    step(v.tensor_copy(raw_t[:, n, :], setup_psum(n)))
                assert done[0] == SETUP_RAW_T
                for n, (dst, vec) in enumerate(scaled_to):
                    step(v.tensor_scalar(dst, setup_psum(n), vecs[:, vec:vec + 1], None, ALU.mult))
                for n, dst in enumerate(copied_to):
                    step(v.tensor_copy(dst, setup_psum(len(scaled_to) + n)))
                dve.wait_ge(setup_pe, 2)
                wait_other_loads(dve)
                dve.wait_ge(setup_mem, N_MEM)
                step(v.tensor_copy(b_q[:, 0:1], ps_q[:, 0:1]))
                step(v.tensor_copy(b_k[:, 0:1], ps_q[:, 1:2]))
                step(v.tensor_copy(b_v[:, 0:1], ps_q[:, 2:3]))
                step(v.tensor_copy(b_q[:, 1:2], ps_q[:, 3:4]))
                step(v.tensor_tensor(b_1[:, 0, :], ps_q[:, 4:8], b_1[:, 0, :], ALU.add))
                settle()
                for i, layer in enumerate((0, 5, 6)):
                    step(v.tensor_copy(b_v_wide[:, i, :], b_v[:, layer:layer + 1].to_broadcast([P, P])))
                assert done[0] == SETUP_WIDE
                for w, w_rot in ((w_q, w_q_rot), (w_k, w_k_rot)):
                    src = w[:, L1_CROSS, :].rearrange("p (h a d) -> p h a d", a=2, d=HD // 2)
                    dst = w_rot[:, :].rearrange("p (h a d) -> p h a d", a=2, d=HD // 2)
                    step(v.tensor_scalar(dst[:, :, 0, :], src[:, :, 1, :], -1.0, None, ALU.mult))
                    step(v.tensor_copy(dst[:, :, 1, :], src[:, :, 0, :]))
                step(v.tensor_copy(ident_bf[:, :], ident[:, :]))
                step(v.tensor_copy(mask_f[:, :], mask_int[:, :]))
                step(v.tensor_scalar(mask_bias[:, 0, :], causal[:, :], -1.0, -MASKED, ALU.add, ALU.mult))
                settle()
                step(v.tensor_tensor(valid[:, :], causal[:, :], mask_f[:, :], ALU.mult))
                settle()
                for i, src in enumerate((valid, mask_f)):
                    step(v.tensor_reduce(row_scale[:, i:i + 1], src[:, :], AX_X, ALU.max))
                settle()
                for i, src in enumerate((valid, mask_f)):
                    step(v.tensor_scalar(src[:, :], src[:, :], -1.0, -MASKED, ALU.add, ALU.mult))
                settle()
                for i, src in enumerate((valid, mask_f)):
                    step(v.tensor_scalar(mask_bias[:, 1 + i, :], src[:, :], row_scale[:, i:i + 1], None,
                                         ALU.mult))
                dve.wait_ge(setup_pe, 3)
                for i, layer in enumerate((0, 5, 6)):
                    step(v.tensor_tensor(b_o_rows[:, layer, :], ps_k[:, i * P:(i + 1) * P],
                                         b_o_rows[:, layer, :], ALU.add))
                assert done[0] == SETUP_DVE, done[0]
                settle()

                def norm_begin(r, j, norm, src, eps, at=0, rms=False):
                    b = j % 2
                    v.bn_stats(norm.stats[:, b, :], src)
                    dve.drain()
                    v.bn_aggr(norm.mean_var[:, b, :], norm.stats[:, b, :]).then_inc(norm.steps.sem, 1)
                    dve.wait_ge(norm.steps.sem, norm.steps.at(r, j, at + 1))
                    var = norm.mean_var[:, b, 1:2]
                    if rms:
                        v.scalar_tensor_tensor(out=norm.mean_sq[:, b:b + 1], in0=norm.mean_var[:, b, 0:1],
                                               scalar=norm.mean_var[:, b, 0:1], in1=var,
                                               op0=ALU.mult, op1=ALU.add).then_inc(norm.steps.sem, 1)
                        dve.wait_ge(norm.steps.sem, norm.steps.at(r, j, at + 2))
                        var = norm.mean_sq[:, b:b + 1]
                    v.tensor_scalar(norm.var_eps[:, b:b + 1], var, eps, None, ALU.add) \
                        .then_inc(norm.steps.sem, 1)

                def post_norm_begin(r, j, norm, which):
                    dve.wait_ge(norm.steps.sem, norm.steps.at(r, j, 1))
                    norm_begin(r, j, norm, x[:, j % STREAMS, :], which[1], at=1)

                def pre_norm_begin(r, j):
                    layer, s = layer_of(j), j % STREAMS
                    if layer not in PRE_NORM:
                        return
                    if layer == L0_SELF:
                        dve.wait_ge(x_loaded[s].sem, load_count(r, j))
                    else:
                        before = last_x_signal(layer_of(j - STREAMS))
                        dve.wait_ge(before.sem, before.at(r, j - STREAMS))
                    norm_begin(r, j, pre_norm, pre_source(j), PRE_NORM[layer], rms=layer == L1_CROSS)

                def mlp_norm_begin(r, j):
                    if layer_of(j) in MLP_PRE_NORM:
                        dve.wait_ge(x_ready.sem, x_ready.at(r, j))
                        norm_begin(r, j, mlp_norm, x[:, j % STREAMS, :], MLP_PRE_NORM[layer_of(j)])

                def pre_k(r, j):
                    layer, s = layer_of(j), j % STREAMS
                    mask = slot_mask[:, :].unsqueeze(2).to_broadcast([P, SLOTS, P])
                    dve.wait_ge(k_ready.sem, k_ready.at(r, j))
                    src = ps_k[:, 0:P]
                    if layer == L1_CROSS:
                        dve.wait_ge(q_ready.sem, q_ready.at(r, j))
                        cos = rope_cos[:, :].unsqueeze(1).to_broadcast([P, 2, LEN])
                        sin = rope_sin[:, :].unsqueeze(1).to_broadcast([P, 2, LEN])

                        def two(t):
                            return t.rearrange("p (b t) -> p b t", b=2)

                        for i, ps in enumerate((ps_q, ps_k)):
                            v.tensor_tensor(two(rope_a[:, i, :]), two(ps[:, 0:P]), cos,
                                            ALU.mult).then_inc(rope_steps.sem, 1)
                            v.tensor_tensor(two(rope_b[:, i, :]), two(ps[:, P:2 * P]), sin,
                                            ALU.mult).then_inc(rope_steps.sem, 1)
                        dve.wait_ge(rope_steps.sem, rope_steps.at(r, j))
                        v.tensor_tensor(rope_qk[:, :, :], rope_a[:, :, :], rope_b[:, :, :],
                                        ALU.add).then_inc(rope_ready.sem, 1)
                        dve.wait_ge(rope_ready.sem, rope_ready.at(r, j))
                        src = rope_qk[:, 1, :]
                    src = src.unsqueeze(1).to_broadcast([P, SLOTS, P])
                    if layer in K_BIAS:
                        ins = v.scalar_tensor_tensor(out=k_slots[:, s, :, :], in0=src,
                                                     scalar=b_k[:, layer:layer + 1], in1=mask,
                                                     op0=ALU.add, op1=ALU.mult)
                    else:
                        ins = v.tensor_tensor(k_slots[:, s, :, :], src, mask, ALU.mult)
                    ins.then_inc(k_slots_ready.sem, 1)

                def shift(r, j, u):
                    layer = layer_of(j)
                    per_half = 2 if layer in ROW_SCALE else 1
                    heads = ps_scores[u][:, :].rearrange("p (h k) -> p h k", k=LEN)
                    dst = shifted[:, u, :].rearrange("p (h k) -> p h k", k=LEN)
                    dve.wait_ge(scores_ready.sem, scores_ready.at(r, j, u + 1))
                    v.tensor_reduce(row_max[:, u, :], heads, AX_X, ALU.max).then_inc(max_done.sem, 1)
                    dve.wait_ge(max_done.sem, max_done.at(r, j, per_half * u + 1))
                    if layer in ROW_SCALE:
                        scale = row_scale[:, ROW_SCALE[layer]:ROW_SCALE[layer] + 1]
                        v.tensor_scalar(scaled_max[:, u, :], row_max[:, u, :], scale, None,
                                        ALU.mult).then_inc(max_done.sem, 1)
                        dve.wait_ge(max_done.sem, max_done.at(r, j, per_half * u + 2))
                        ins = v.scalar_tensor_tensor(
                            out=dst, in0=heads, scalar=scale,
                            in1=scaled_max[:, u, :].unsqueeze(2).to_broadcast([P, 8, LEN]),
                            op0=ALU.mult, op1=ALU.subtract)
                    else:
                        ins = v.tensor_tensor(dst, heads, row_max[:, u, :].unsqueeze(2)
                                              .to_broadcast([P, 8, LEN]), ALU.subtract)
                    ins.then_inc(shifted_ready.sem, 1)

                def normalise(r, j):
                    dve.wait_ge(pv_t_ready.sem, pv_t_ready.at(r, j))
                    view = ps_post[:, 256:512].rearrange("p (h w e d) -> p h w e d", w=2, e=2, d=HD)
                    v.reciprocal(recip[:, :].rearrange("p (h e) -> p h e", e=2),
                                 view[:, :, 1, :, 0]).then_inc(recip_done.sem, 1)
                    dve.wait_ge(recip_done.sem, recip_done.at(r, j))
                    v.tensor_tensor(attn[:, :].rearrange("p (h e d) -> p h e d", e=2, d=HD), view[:, :, 0, :, :],
                                    recip[:, :].rearrange("p (h e) -> p h e", e=2).unsqueeze(3)
                                    .to_broadcast([P, HEADS // 2, 2, HD]), ALU.mult).then_inc(attn_ready.sem, 1)

                def residual(r, j):
                    layer, s = layer_of(j), j % STREAMS
                    dve.wait_ge(y_ready.sem, y_ready.at(r, j))
                    dve.wait_ge(x_bias_ready.sem, x_bias_ready.at(r, j))
                    if layer == L0_SELF:
                        dve.wait_ge(stored[s].sem, r * 16 + 16 * (j // PER_ROUND) + STORED_0)
                    after = post_steps if layer in POST_NORM else x_ready
                    v.tensor_tensor(x[:, s, :], ps_post[:, P:2 * P], x_bias[:, s, :],
                                    ALU.add).then_inc(after.sem, 1)
                    if layer in POST_NORM:
                        post_norm_begin(r, j, post_norm, POST_NORM[layer])

                def mlp_residual(r, j):
                    layer, s = layer_of(j), j % STREAMS
                    dve.wait_ge(mlp_y_ready.sem, mlp_y_ready.at(r, j))
                    dve.wait_ge(mlp_x_bias_ready.sem, mlp_x_bias_ready.at(r, j))
                    after = mlp_post_steps if layer in MLP_POST_NORM else mlp_x_ready
                    v.tensor_tensor(x[:, s, :], ps_k[:, 256:384], x_bias[:, s, :],
                                    ALU.add).then_inc(after.sem, 1)
                    if layer in MLP_POST_NORM:
                        post_norm_begin(r, j, mlp_post_norm, MLP_POST_NORM[layer])

                def phase(r, j):
                    core, post, pre = exists(r, j), exists(r, j - 1), exists(r, j + PRE)
                    down = has_mlp(r, j - DOWN)
                    if core:
                        shift(r, j, 0)
                    if post:
                        normalise(r, j - 1)
                    if core:
                        shift(r, j, 1)
                    if down:
                        mlp_residual(r, j - DOWN)
                    if pre:
                        pre_k(r, j + PRE)
                    if post:
                        residual(r, j - 1)
                    if has_mlp(r, j - UP + 1):
                        mlp_norm_begin(r, j - UP + 1)
                    if exists(r, j + PRE + 1):
                        pre_norm_begin(r, j + PRE + 1)

                rounds(dve, phase)


SETUP_RAW_T = 8
SETUP_WIDE = SETUP_RAW_T + 9 + 11 + 5 + 3
SETUP_DVE = SETUP_WIDE + 4 + 4 + 6 + 3


def constants():
    c = np.arange(P)
    half = HD // 2
    inv_freq = (np.float32(1.0) / np.float32(10000.0) ** (np.arange(half, dtype=np.float32) / np.float32(half))).astype(np.float32)
    angle = (np.arange(LEN, dtype=np.float32)[None, :] * inv_freq[(c % half)][:, None]).astype(np.float32)
    return {
        "c_ident": np.eye(P, dtype=np.float32),
        "c_slot": ((c[:, None] // HD) % SLOTS == np.arange(SLOTS)[None, :]).astype(np.float32),
        "c_causal": ((c[:, None] % LEN) >= np.arange(LEN)[None, :]).astype(np.float32),
        "c_cos": np.cos(angle).astype(np.float32),
        "c_sin": np.sin(angle).astype(np.float32),
    }


def kernel(**inputs):
    import concourse.bacc as bacc
    from concourse.bass_utils import run_bass_kernel_spmd

    nc = bacc.Bacc("TRN2", target_bir_lowering=False, num_devices=1)
    arrays, aps = {}, {}
    for name, value in {**inputs, **constants()}.items():
        value = np.ascontiguousarray(value)
        arrays[f"in_{name}"] = value
        aps[name] = nc.dram_tensor(f"in_{name}", value.shape, mybir.dt.from_np(value.dtype),
                                   kind="ExternalInput").ap()
    out = nc.dram_tensor("out_0", (SEQS, LEN, DIM), F32, kind="ExternalOutput").ap()
    build(nc, aps, out)
    result = run_bass_kernel_spmd(nc, [arrays], core_ids=[0])
    return result.results[0]["out_0"]
```
